# Optimizing a Trainium2 kernel written in Bass

```python
import numpy as np
import jax
import jax.numpy as jnp

def _softmax(x, axis=-1):
    return jax.nn.softmax(x, axis=axis)

def _gelu(x):
    return jax.nn.gelu(x, approximate=True)

def _silu(x):
    return jax.nn.silu(x)

def _sigmoid(x):
    return jax.nn.sigmoid(x)

def _layernorm(x, axis=-1, eps=1e-05):
    m = jnp.mean(x, axis=axis, keepdims=True)
    v = jnp.var(x, axis=axis, keepdims=True)
    return (x - m) / jnp.sqrt(v + eps)

def _scatter_add(tgt, idx, src, axis=0):
    return tgt.at[idx].add(src)

def _segment_sum(src, seg, n):
    return jax.ops.segment_sum(src, seg, n)
kernel_name = 'mk_macaron_d1_jaxref_r8_0ead74'

def setup_inputs(seed: int=0):
    np.random.seed(seed)
    _w = jnp.asarray

    def _L0_attn_setup():
        import jax, jax.numpy as jnp
        import numpy as np
        D_MODEL = 128
        EXPAND = 2
        D_STATE = 128
        D_CONV = 4
        HEADDIM = 64
        CHUNK = 64
        D_INNER = EXPAND * D_MODEL
        NHEADS = D_INNER // HEADDIM
        CONV_DIM = D_INNER + 2 * D_STATE
        D_IN_PROJ = 2 * D_INNER + 2 * D_STATE + NHEADS
        EPS = 1e-05

        def _segsum(a):
            T = a.shape[-1]
            cs = jnp.cumsum(a, -1)
            ss = cs[..., :, None] - cs[..., None, :]
            mask = jnp.tril(jnp.ones((T, T), dtype=bool))
            return jnp.where(mask, ss, -jnp.inf)

        def _ssd(xdt, A, Bm, Cm):
            b, l, h, p = xdt.shape
            c = l // CHUNK
            xr = xdt.reshape(b, c, CHUNK, h, p)
            Ar = A.reshape(b, c, CHUNK, h).transpose(0, 3, 1, 2)
            Br = Bm.reshape(b, c, CHUNK, -1)
            Cr = Cm.reshape(b, c, CHUNK, -1)
            Acs = jnp.cumsum(Ar, -1)
            Lmat = jnp.exp(_segsum(Ar))
            Y_diag = jnp.einsum('bcln,bcsn,bhcls,bcshp->bclhp', Cr, Br, Lmat, xr)
            decay_states = jnp.exp(Acs[..., -1:] - Acs)
            states = jnp.einsum('bcln,bhcl,bclhp->bchpn', Br, decay_states, xr)
            A_last = jnp.pad(Acs[..., -1], ((0, 0), (0, 0), (1, 0)))
            decay_chunk = jnp.exp(_segsum(A_last))
            states = jnp.concatenate([jnp.zeros_like(states[:, :1]), states], axis=1)
            new_states = jnp.einsum('bhzc,bchpn->bzhpn', decay_chunk, states)
            prev = new_states[:, :-1]
            Y_off = jnp.einsum('bcln,bchpn,bhcl->bclhp', Cr, prev, jnp.exp(Acs))
            return (Y_diag + Y_off).reshape(b, l, h, p)
        key = jax.random.key(seed)
        ks = jax.random.split(key, 8)
        B, L = (4, 256)
        x = jax.random.normal(ks[0], (B, L, D_MODEL), dtype=jnp.float32)
        W_in = jax.random.normal(ks[1], (D_IN_PROJ, D_MODEL), dtype=jnp.float32) * 0.02
        conv_w = jax.random.normal(ks[2], (CONV_DIM, D_CONV), dtype=jnp.float32) * 0.2
        conv_b = jax.random.normal(ks[3], (CONV_DIM,), dtype=jnp.float32) * 0.02
        dt = jax.random.uniform(ks[4], (NHEADS,), minval=0.001, maxval=0.1)
        dt_bias = (dt + jnp.log(-jnp.expm1(-dt))).astype(jnp.float32)
        A_log = jnp.log(jax.random.uniform(ks[5], (NHEADS,), minval=1.0, maxval=16.0)).astype(jnp.float32)
        Dskip = jnp.ones((NHEADS,), dtype=jnp.float32)
        norm_w = jnp.ones((D_INNER,), dtype=jnp.float32)
        W_out = jax.random.normal(ks[6], (D_MODEL, D_INNER), dtype=jnp.float32) * 0.02
        ln_g = jnp.ones((D_MODEL,), dtype=jnp.float32)
        ln_b = jnp.zeros((D_MODEL,), dtype=jnp.float32)
        return {'x': x, 'W_in': W_in, 'conv_w': conv_w, 'conv_b': conv_b, 'dt_bias': dt_bias, 'A_log': A_log, 'Dskip': Dskip, 'norm_w': norm_w, 'W_out': W_out, 'ln_g': ln_g, 'ln_b': ln_b}
    _L0_attn_in = _L0_attn_setup()

    def _L0_ffn_setup():
        import jax, jax.numpy as jnp
        import numpy as np
        HIDDEN = 128
        NUM_EXPERTS = 8
        TOP_K = 2
        B, S = (4, 128)
        key = jax.random.key(seed)
        ks = jax.random.split(key, 8)
        H, E = (HIDDEN, NUM_EXPERTS)
        sc = lambda fan_in: 1.0 / np.sqrt(fan_in)
        x = jax.random.normal(ks[0], (B, S, H), dtype=jnp.float32)
        Wr = jax.random.uniform(ks[1], (H, E), minval=-sc(H), maxval=sc(H), dtype=jnp.float32)
        br = jax.random.uniform(ks[2], (E,), minval=-sc(H), maxval=sc(H), dtype=jnp.float32)
        W1 = jax.random.uniform(ks[3], (E, H, 2 * H), minval=-sc(H), maxval=sc(H), dtype=jnp.float32)
        b1 = jax.random.uniform(ks[4], (E, 2 * H), minval=-sc(H), maxval=sc(H), dtype=jnp.float32)
        W2 = jax.random.uniform(ks[5], (E, 2 * H, H), minval=-sc(2 * H), maxval=sc(2 * H), dtype=jnp.float32)
        b2 = jax.random.uniform(ks[6], (E, H), minval=-sc(2 * H), maxval=sc(2 * H), dtype=jnp.float32)
        return {'x': x, 'Wr': Wr, 'br': br, 'W1': W1, 'b1': b1, 'W2': W2, 'b2': b2}
    _L0_ffn_in = _L0_ffn_setup()
    _d = {'L0_attn_x': _L0_attn_in['x'], 'L0_attn_W_in': _L0_attn_in['W_in'], 'L0_attn_conv_w': _L0_attn_in['conv_w'], 'L0_attn_conv_b': _L0_attn_in['conv_b'], 'L0_attn_dt_bias': _L0_attn_in['dt_bias'], 'L0_attn_A_log': _L0_attn_in['A_log'], 'L0_attn_Dskip': _L0_attn_in['Dskip'], 'L0_attn_norm_w': _L0_attn_in['norm_w'], 'L0_attn_W_out': _L0_attn_in['W_out'], 'L0_attn_ln_g': _L0_attn_in['ln_g'], 'L0_attn_ln_b': _L0_attn_in['ln_b'], 'L0_ffn_Wr': _L0_ffn_in['Wr'], 'L0_ffn_br': _L0_ffn_in['br'], 'L0_ffn_W1': _L0_ffn_in['W1'], 'L0_ffn_b1': _L0_ffn_in['b1'], 'L0_ffn_W2': _L0_ffn_in['W2'], 'L0_ffn_b2': _L0_ffn_in['b2']}
    _x0 = _d['L0_attn_x']
    _d['L0_attn_x'] = jax.random.normal(jax.random.fold_in(jax.random.key(seed), 1), (32, 256, 128), dtype=_x0.dtype)
    del _x0
    return _d

def reference(L0_attn_x, L0_attn_W_in, L0_attn_conv_w, L0_attn_conv_b, L0_attn_dt_bias, L0_attn_A_log, L0_attn_Dskip, L0_attn_norm_w, L0_attn_W_out, L0_attn_ln_g, L0_attn_ln_b, L0_ffn_Wr, L0_ffn_br, L0_ffn_W1, L0_ffn_b1, L0_ffn_W2, L0_ffn_b2):

    def _L0_attn_ref(x, W_in, conv_w, conv_b, dt_bias, A_log, Dskip, norm_w, W_out, ln_g, ln_b):
        import jax, jax.numpy as jnp
        import numpy as np
        D_MODEL = 128
        EXPAND = 2
        D_STATE = 128
        D_CONV = 4
        HEADDIM = 64
        CHUNK = 64
        D_INNER = EXPAND * D_MODEL
        NHEADS = D_INNER // HEADDIM
        CONV_DIM = D_INNER + 2 * D_STATE
        D_IN_PROJ = 2 * D_INNER + 2 * D_STATE + NHEADS
        EPS = 1e-05

        def _segsum(a):
            T = a.shape[-1]
            cs = jnp.cumsum(a, -1)
            ss = cs[..., :, None] - cs[..., None, :]
            mask = jnp.tril(jnp.ones((T, T), dtype=bool))
            return jnp.where(mask, ss, -jnp.inf)

        def _ssd(xdt, A, Bm, Cm):
            b, l, h, p = xdt.shape
            c = l // CHUNK
            xr = xdt.reshape(b, c, CHUNK, h, p)
            Ar = A.reshape(b, c, CHUNK, h).transpose(0, 3, 1, 2)
            Br = Bm.reshape(b, c, CHUNK, -1)
            Cr = Cm.reshape(b, c, CHUNK, -1)
            Acs = jnp.cumsum(Ar, -1)
            Lmat = jnp.exp(_segsum(Ar))
            Y_diag = jnp.einsum('bcln,bcsn,bhcls,bcshp->bclhp', Cr, Br, Lmat, xr)
            decay_states = jnp.exp(Acs[..., -1:] - Acs)
            states = jnp.einsum('bcln,bhcl,bclhp->bchpn', Br, decay_states, xr)
            A_last = jnp.pad(Acs[..., -1], ((0, 0), (0, 0), (1, 0)))
            decay_chunk = jnp.exp(_segsum(A_last))
            states = jnp.concatenate([jnp.zeros_like(states[:, :1]), states], axis=1)
            new_states = jnp.einsum('bhzc,bchpn->bzhpn', decay_chunk, states)
            prev = new_states[:, :-1]
            Y_off = jnp.einsum('bcln,bchpn,bhcl->bclhp', Cr, prev, jnp.exp(Acs))
            return (Y_diag + Y_off).reshape(b, l, h, p)
        B, L, _ = x.shape
        mu = jnp.mean(x, -1, keepdims=True)
        var = jnp.mean((x - mu) ** 2, -1, keepdims=True)
        xn = (x - mu) * jax.lax.rsqrt(var + EPS) * ln_g + ln_b
        zxbcdt = xn @ W_in.T
        z = zxbcdt[..., :D_INNER]
        xBC = zxbcdt[..., D_INNER:D_INNER + CONV_DIM]
        dt_raw = zxbcdt[..., D_INNER + CONV_DIM:]
        xp = jnp.pad(xBC, ((0, 0), (D_CONV - 1, 0), (0, 0)))
        conv = conv_b + sum((xp[:, k:k + L, :] * conv_w[:, k] for k in range(D_CONV)))
        xBC = jax.nn.silu(conv)
        xs = xBC[..., :D_INNER]
        Bm = xBC[..., D_INNER:D_INNER + D_STATE]
        Cm = xBC[..., D_INNER + D_STATE:]
        dt = jax.nn.softplus(dt_raw + dt_bias)
        A = -jnp.exp(A_log)
        xh = xs.reshape(B, L, NHEADS, HEADDIM)
        y = _ssd(xh * dt[..., None], dt * A, Bm, Cm)
        y = y + Dskip[None, None, :, None] * xh
        y = y.reshape(B, L, D_INNER)
        y = y * jax.nn.silu(z)
        y = y * jax.lax.rsqrt(jnp.mean(y * y, -1, keepdims=True) + EPS) * norm_w
        y = y @ W_out.T
        return y + x

    def _L0_ffn_ref(x, Wr, br, W1, b1, W2, b2):
        import jax, jax.numpy as jnp
        import numpy as np
        HIDDEN = 128
        NUM_EXPERTS = 8
        TOP_K = 2
        B, S = (4, 128)
        B_, S_, H = x.shape
        xf = x.reshape(-1, H)
        logits = xf @ Wr + br
        topk_w, topk_idx = jax.lax.top_k(logits, TOP_K)
        topk_w = jax.nn.softmax(topk_w, axis=-1)
        gate = jnp.sum(jax.nn.one_hot(topk_idx, NUM_EXPERTS, dtype=xf.dtype) * topk_w[..., None], axis=1)
        h = jax.nn.relu(jnp.einsum('th,ehf->etf', xf, W1) + b1[:, None, :])
        y = jnp.einsum('etf,efh->eth', h, W2) + b2[:, None, :]
        out = jnp.einsum('te,eth->th', gate, y)
        return out.reshape(B_, S_, H)
    x = L0_attn_x
    x = x + 0.5 * _L0_ffn_ref(_layernorm(x, axis=-1), L0_ffn_Wr, L0_ffn_br, L0_ffn_W1, L0_ffn_b1, L0_ffn_W2, L0_ffn_b2)
    x = x + _L0_attn_ref(_layernorm(x, axis=-1), L0_attn_W_in, L0_attn_conv_w, L0_attn_conv_b, L0_attn_dt_bias, L0_attn_A_log, L0_attn_Dskip, L0_attn_norm_w, L0_attn_W_out, L0_attn_ln_g, L0_attn_ln_b)
    x = x + 0.5 * _L0_ffn_ref(_layernorm(x, axis=-1), L0_ffn_Wr, L0_ffn_br, L0_ffn_W1, L0_ffn_b1, L0_ffn_W2, L0_ffn_b2)
    return x

_drawn_inputs = setup_inputs


def setup_inputs(seed=0):
    import zlib

    import numpy as np

    out = dict(_drawn_inputs(seed))
    spreads = {'L0_attn_Dskip': (1.0, 0.2),
     'L0_attn_norm_w': (1.0, 0.577),
     'L0_attn_ln_g': (1.0, 0.2),
     'L0_attn_ln_b': (0.0, 0.386)}
    factors = {'L0_attn_dt_bias': 8.0, 'L0_attn_A_log': 8.0, 'L0_ffn_b1': 5.118, 'L0_ffn_b2': 2.844}
    for name, (base, spread) in spreads.items():
        noise = np.random.default_rng([zlib.crc32(name.encode()), seed]).standard_normal(out[name].shape)
        drawn = base * np.exp(spread * noise) if base else spread * noise
        out[name] = jnp.asarray(drawn.astype(out[name].dtype))
    for name, factor in factors.items():
        out[name] = (out[name] * factor).astype(out[name].dtype)
    return out
```

```python
from contextlib import ExitStack

import concourse.bass as bass
from concourse import mybir

ALU = mybir.AluOpType
ACT = mybir.ActivationFunctionType
AX = mybir.AxisListType
F32 = mybir.dt.float32
BF16 = mybir.dt.bfloat16
I32 = mybir.dt.int32

P = 128
D = 128
D_INNER = 256
NHEADS = 4
HEADDIM = D_INNER // NHEADS
NSTATE = 128
D_CONV = 4
NEXP = 8
FF = 256
EPS = 1e-5

SEQ = 256
CH = SEQ // P
BW = 4
TW = BW * CH
ROWS_BOUND = (2 * TW * P + NEXP * (P - 1)) // P
RING = 4
NB = -(-ROWS_BOUND // RING) * RING
PER_SLOT = NB // RING
ROUNDS = PER_SLOT - 1
TAIL = RING * ROUNDS
ZCOL, XCOL, DTCOL = 0, D_INNER, 2 * D_INNER + 2 * NSTATE
NPROJ = DTCOL + NHEADS
MAGIC = 0x5F3759DF
HUGE = 3.0e38


class Chain:

    def __init__(self, eng, sem, base):
        self.eng, self.sem, self.base, self.k = eng, sem, base, 0

    def mark(self, ins):
        ins.then_inc(self.sem, 1)
        self.k += 1

    def settle(self):
        self.eng.wait_ge(self.sem, self.base + self.k)

    def link(self, ins):
        self.mark(ins)
        self.settle()


RSQRT_STEPS = 12
DISPATCH_STEPS = 2 * TW + 1 + RSQRT_STEPS + 30
MIX0_STEPS = 3 * TW + 2 * RSQRT_STEPS + 17
MIX1_STEPS = 2 * BW + 1 + RSQRT_STEPS
COMBINE_STEPS = TW


def build_program(nc, x, w_in_t, conv_w, conv_b, dt_bias, a_log, dskip, norm_w, w_out_t,
                  ln_g, ln_b, wr, br, w1, b1, w2, b2, out):
    n_seq = x.shape[0]
    NT = n_seq * SEQ // P
    NW = NT // TW
    assert NT == NW * TW

    x_rows = x.rearrange("b (c p) d -> p (b c) d", p=P)
    out_rows = out.rearrange("b (c p) d -> p (b c) d", p=P)
    sorted_in = [nc.dram_tensor(f"sorted_in{p}", [NB * P, D], F32, kind="Internal").ap() for p in range(2)]
    sorted_out = [nc.dram_tensor(f"sorted_out{p}", [NB * P, D], F32, kind="Internal").ap() for p in range(2)]
    cs_dram = nc.dram_tensor("cs_rows", [CH * BW * NHEADS, P], F32, kind="Internal").ap()

    with ExitStack() as ctx:
        def sb(name, shape, dt=F32):
            return ctx.enter_context(nc.sbuf_tensor(name, shape, dt))

        def sem(name):
            return ctx.enter_context(nc.semaphore(name))

        ident = sb("ident", [P, P])
        upper = sb("upper", [P, P])
        below_bf = sb("below_bf", [P, P], BF16)
        ones = sb("ones", [P, P])
        ones_bf = sb("ones_bf", [P, P], BF16)
        causal = sb("causal", [P, 3, P])
        expert_rev = sb("expert_rev", [P, TW, NEXP])
        tile_start = sb("tile_start", [P, NEXP, TW])
        block_no = sb("block_no", [1, NB, NEXP])
        not_first = sb("not_first", [P, NEXP, TW])
        itmp = sb("itmp", [P, NB * NEXP], I32)
        w_in_sb = sb("w_in_sb", [P, NPROJ])
        w_out_sb = sb("w_out_sb", [P, 2, D])
        conv_w_sb = sb("conv_w_sb", [P, 4, D_CONV])
        conv_b_sb = sb("conv_b_sb", [P, 4])
        dtb_sb = sb("dtb_sb", [P, NHEADS])
        aneg_sb = sb("aneg_sb", [P, NHEADS])
        dskip_sb = sb("dskip_sb", [P, 2])
        normw_sb = sb("normw_sb", [P, 2])
        lng_sb = sb("lng_sb", [P, 1])
        lnb_sb = sb("lnb_sb", [P, 1])
        wr_pad = sb("wr_pad", [P, 64])
        br_sb = sb("br_sb", [P, NEXP])
        w1_sb = sb("w1_sb", [P, NEXP, FF + 2])
        w2_sb = sb("w2_sb", [P, 2 * NEXP, D])
        b2_sb = sb("b2_sb", [P, NEXP, D])

        X = sb("X", [P, NT, D])
        stats = sb("stats", [P, TW, 6])
        mv = sb("mv", [P, TW, 2])
        rs_v = sb("rs_v", [P, TW])
        rs_i = sb("rs_i", [P, TW], I32)
        rs_h = sb("rs_h", [P, TW])
        rs_t = sb("rs_t", [P, TW])
        rs_y = sb("rs_y", [P, TW], I32)
        xn = sb("xn", [P, 2, TW, D])
        xnT = sb("xnT", [P, TW * P])
        lg = sb("lg", [P, TW, NEXP])
        lg2 = sb("lg2", [P, TW, NEXP])
        sc = sb("sc", [P, TW, NEXP])
        oh = sb("oh", [P, 2, TW, NEXP])
        chosen = sb("chosen", [P, TW, NEXP], BF16)
        mx = sb("mx", [P, 4, TW])
        dm = sb("dm", [P, TW])
        ex = sb("ex", [P, TW])
        incl = sb("incl", [P, NEXP, TW])
        rank = sb("rank", [P, NEXP, TW])
        cmp = sb("cmp", [P, NEXP, TW])
        nblk = sb("nblk", [P, NEXP])
        bend = sb("bend", [P, NEXP])
        bstart = sb("bstart", [P, NEXP])
        bcmp = sb("bcmp", [1, NB, NEXP])
        bsum = sb("bsum", [1, NB])
        pos = sb("pos", [P, 2, TW])
        idx = sb("idx", [P, 2, 2, TW], I32)
        gate = sb("gate", [P, 2, 2, TW])
        block_expert = sb("block_expert", [1, 2, NB], I32)

        xb = sb("xb", [P, RING, D])
        w1b = sb("w1b", [P, RING, FF + 2])
        xbT = sb("xbT", [P, 2, P])
        hb = sb("hb", [P, 2, 2, P])
        yb = sb("yb", [P, RING, D])
        yg = sb("yg", [P, 2, TW, D])

        un = sb("un", [P, TW, D])
        unT = sb("unT", [P, TW * P])
        r1 = sb("r1", [P, TW])
        dtx = sb("dtx", [P, CH, BW, NHEADS])
        dta = sb("dta", [P, CH, BW, NHEADS])
        dte = sb("dte", [P, CH, BW, NHEADS])
        dtu = sb("dtu", [P, CH, BW, NHEADS])
        dtl = sb("dtl", [P, CH, BW, NHEADS])
        dtr = sb("dtr", [P, CH, BW, NHEADS])
        dt_t = sb("dt_t", [P, CH, BW, NHEADS])
        a_t = sb("a_t", [P, CH, BW, NHEADS])
        cs_t = sb("cs_t", [P, CH * BW * NHEADS])
        ncs_t = sb("ncs_t", [P, CH, BW, NHEADS])
        cs_r = sb("cs_r", [CH * BW * NHEADS, P])
        csb = sb("csb", [P, CH, BW * NHEADS, P])
        acc = sb("acc", [P, 2, 2 * SEQ])
        xbc = sb("xbc", [P, 4, BW * SEQ])
        zs = sb("zs", [P, 2, BW * SEQ])
        xdt = sb("xdt", [P, 2, CH, NHEADS, HEADDIM])
        gm = sb("gm", [P, 2, 3, P])
        decay = sb("decay", [P, 2, 3 * NHEADS * P])
        mix = sb("mix", [P, 2, 3 * NHEADS * P])
        yz = sb("yz", [P, 2, 2, SEQ])
        sq = sb("sq", [P, 2, 2, SEQ])
        ss = sb("ss", [P, 2, SEQ])

        bank = [ctx.enter_context(nc.psum_tensor(f"bank{i}", [P, 512], F32)) for i in range(8)]

        weights_loaded = sem("weights_loaded")
        pool_consts = sem("pool_consts")
        pool_fill = sem("pool_fill")
        sorted_zeroed = sem("sorted_zeroed")
        fixed_dve = sem("fixed_dve")
        fixed_act = sem("fixed_act")
        x_loaded = sem("x_loaded")
        d_chain = sem("d_chain")
        d_xn = sem("d_xn")
        d_T = sem("d_T")
        d_xT = sem("d_xT")
        d_logits = sem("d_logits")
        d_margin = sem("d_margin")
        d_exp = sem("d_exp")
        d_chosen = sem("d_chosen")
        d_rank = sem("d_rank")
        d_plan = sem("d_plan")
        scattered = [sem(f"scattered{p}") for p in range(2)]
        w1_loaded = [sem(f"w1_loaded{s}") for s in range(RING)]
        xb_loaded = [sem(f"xb_loaded{s}") for s in range(RING)]
        y_stored = [sem(f"y_stored{s}") for s in range(RING)]
        e_T = sem("e_T")
        e_xT = sem("e_xT")
        e_H = sem("e_H")
        e_h = sem("e_h")
        e_Y = sem("e_Y")
        e_y = sem("e_y")
        gathered = sem("gathered")
        c_chain = sem("c_chain")
        c_x = sem("c_x")
        out_stored = sem("out_stored")
        m_chain = sem("m_chain")
        m_u = sem("m_u")
        m_T = sem("m_T")
        m_uT = sem("m_uT")
        m_dt = sem("m_dt")
        m_abs = sem("m_abs")
        m_exp = sem("m_exp")
        m_one = sem("m_one")
        m_log = sem("m_log")
        m_a = sem("m_a")
        m_cs = sem("m_cs")
        m_cst = sem("m_cst")
        m_csT = sem("m_csT")
        m_csr = sem("m_csr")
        cs_stored = sem("cs_stored")
        cs_loaded = sem("cs_loaded")
        p_xbc = sem("p_xbc")
        p_z = sem("p_z")
        p_acc = sem("p_acc")
        p_tap = sem("p_tap")
        p_chain = sem("p_chain")
        p_silu = sem("p_silu")
        p_zs = sem("p_zs")
        b_chain = sem("b_chain")
        c2_chain = sem("c2_chain")
        sp_past = sem("sp_past")
        pool_past = sem("pool_past")
        dve_past = sem("dve_past")
        b_T = sem("b_T")
        b_G = sem("b_G")
        b_xdt = sem("b_xdt")
        b_gm = sem("b_gm")
        b_decay = sem("b_decay")
        b_mix = sem("b_mix")
        b_Y = sem("b_Y")
        b_yz = sem("b_yz")
        b_sq = sem("b_sq")
        b_ss = sem("b_ss")
        b_O = sem("b_O")
        b_x = sem("b_x")

        WEIGHT_DMAS = 20
        POOL_CONSTS = 11

        def consts_ready(eng):
            eng.wait_ge(weights_loaded, 16 * WEIGHT_DMAS)
            eng.wait_ge(pool_consts, POOL_CONSTS)
            eng.wait_ge(fixed_dve, 7)
            eng.wait_ge(fixed_act, 1)

        def step_past(eng, marker):
            eng.sem_inc(marker, 1)

        def decay_view(s):
            first = s[:, 0:NHEADS * SEQ].rearrange("p (h l) -> p h l", h=NHEADS)
            second = s[:, NHEADS * SEQ:].rearrange("p (h l) -> p h l", h=NHEADS)
            return first, second

        block = ctx.enter_context(nc.Block())

        @block.sync
        def _(sp):
            loads = [
                (w_in_sb[:], w_in_t), (w_out_sb[:], w_out_t.rearrange("(m p) n -> p m n", p=P)),
                (conv_w_sb[:], conv_w), (conv_b_sb[:], conv_b),
                (dtb_sb[:], dt_bias.partition_broadcast(P)), (aneg_sb[:], a_log.partition_broadcast(P)),
                (normw_sb[:], norm_w), (lng_sb[:], ln_g), (lnb_sb[:], ln_b),
                (br_sb[:], br.partition_broadcast(P)), (wr_pad[:, 0:NEXP], wr),
                (w1_sb[:, :, 0:FF], w1.rearrange("e h f -> h e f")), (w1_sb[:, :, FF:FF + 2], b1),
                (w2_sb[:], w2.rearrange("e (m p) n -> p (e m) n", p=P)),
                (b2_sb[:], b2.partition_broadcast(P)),
            ]
            sp.wait_ge(pool_fill, 1)
            for dst, src in loads:
                sp.dma_start(dst, src).then_inc(weights_loaded, 16)
            for g in range(2):
                sp.dma_start(dskip_sb[64 * g:64 * g + 64, :], dskip[g].partition_broadcast(64)).then_inc(weights_loaded, 16)
            for _ in range(WEIGHT_DMAS - len(loads) - 2):
                sp.sem_inc(weights_loaded, 16)
            sp.wait_ge(pool_fill, 2)
            zero = yg[:].rearrange("p k i d -> p (k i) d")
            for p in range(2):
                rows = sorted_in[p].rearrange("(k p) d -> p k d", p=P)
                for a in range(0, NB, 2 * TW):
                    k = min(2 * TW, NB - a)
                    sp.dma_start(rows[:, a:a + k, :], zero[:, 0:k, :]).then_inc(sorted_zeroed, 16)

            def wait_sp(semaphore, value):
                sp.wait_ge(semaphore, value)
                step_past(sp, sp_past)

            def expert(n, w, p):
                wait_sp(d_plan, n + 1)
                wait_sp(scattered[p], 256 * (w + 1))
                wait_sp(gathered, 256 * n)

                def load(b, s):
                    e = sp.value_load(block_expert[0:1, p, bass.ds(b, 1)], min_val=0, max_val=NEXP - 1)
                    sp.dma_start(xb[:, s, :], sorted_in[p][bass.ds(b * P, P), :]).then_inc(xb_loaded[s], 16)
                    sp.dma_start(w1b[:, s, :], w1_sb[:, bass.ds(e, 1), :]).then_inc(w1_loaded[s], 16)

                def store(b, s):
                    wait_sp(e_y, n * NB + b + 1)
                    sp.dma_start(sorted_out[p][bass.ds(b * P, P), :], yb[:, s, :]).then_inc(y_stored[s], 16)

                for b in range(RING):
                    load(b, b)
                with sp.Fori(0, ROUNDS) as r:
                    for s in range(RING):
                        wait_sp(e_h, n * NB + r * RING + s + 1)
                        load(r * RING + s + RING, s)
                        store(r * RING + s, s)
                for b in range(TAIL, NB):
                    store(b, b % RING)

            with sp.Fori(0, NW) as w:
                sp.dma_start(X[:, bass.ds(w * TW, TW), :], x_rows[:, bass.ds(w * TW, TW), :]).then_inc(x_loaded, 16)
                expert(2 * w, w, 0)
                wait_sp(m_csr, w + 1)
                sp.dma_start(cs_dram, cs_r[:]).then_inc(cs_stored, 16)
                wait_sp(cs_stored, 16 * (w + 1))
                sp.dma_start(csb[:].rearrange("p c k l -> p (c k l)"),
                             cs_dram.rearrange("r l -> (r l)").partition_broadcast(P)).then_inc(cs_loaded, 16)
                expert(2 * w + 1, w, 1)
                wait_sp(c_x, TW * (2 * w + 2))
                sp.dma_start(out_rows[:, bass.ds(w * TW, TW), :], X[:, bass.ds(w * TW, TW), :]).then_inc(out_stored, 16)
            sp.wait_ge(out_stored, 16 * NW)

        @block.gpsimd
        def _(pool):
            pool.memset(wr_pad[:], 0.0).then_inc(pool_fill, 1)
            pool.memset(yg[:], 0.0).then_inc(pool_fill, 1)
            pool.memset(ident[:], 0.0).then_inc(pool_consts, 1)
            pool.memset(ones[:], 1.0).then_inc(pool_consts, 1)
            pool.memset(ones_bf[:], 1.0).then_inc(pool_consts, 1)
            pool.memset(causal[:, 1, :], 1.0).then_inc(pool_consts, 1)
            pool.wait_ge(pool_consts, 4)
            pool.affine_select(out=ident[:], in_=ident[:], compare_op=ALU.not_equal, fill=1.0, base=0,
                               pattern=[[-1, P]], channel_multiplier=1).then_inc(pool_consts, 1)
            for dst in (upper[:], causal[:, 0, :], causal[:, 2, :]):
                pool.affine_select(out=dst, in_=ones[:], compare_op=ALU.is_ge, fill=0.0, base=0,
                                   pattern=[[1, P]], channel_multiplier=-1).then_inc(pool_consts, 1)
            pool.affine_select(out=below_bf[:], in_=ones_bf[:], compare_op=ALU.is_ge, fill=0.0, base=-1,
                               pattern=[[1, P]], channel_multiplier=-1).then_inc(pool_consts, 1)

            def count(dst, parts, base, pattern, n):
                if n:
                    pool.wait_ge(pool_fill, 2 + 2 * n)
                pool.iota(itmp[0:parts, 0:dst.free_size()], pattern=pattern, base=base,
                          channel_multiplier=0).then_inc(pool_fill, 1)
                pool.wait_ge(pool_fill, 3 + 2 * n)
                pool.tensor_copy(dst, itmp[0:parts, 0:dst.free_size()]).then_inc(pool_fill, 1)

            count(expert_rev[:].rearrange("p i e -> p (i e)"), P, NEXP, [[0, TW], [-1, NEXP]], 0)
            count(tile_start[:].rearrange("p e j -> p (e j)"), P, 0, [[0, NEXP], [P, TW]], 1)
            count(block_no[:].rearrange("p k e -> p (k e)"), 1, 0, [[1, NB], [0, NEXP]], 2)
            pool.memset(not_first[:], 1.0).then_inc(pool_fill, 1)
            pool.wait_ge(pool_fill, 9)
            pool.memset(not_first[:, :, 0:1], 0.0).then_inc(pool_consts, 1)
            pool.wait_ge(sorted_zeroed, 16 * 2 * -(-NB // (2 * TW)))
            pool.sem_inc(pool_consts, 1)

            def scatter(n, w, p):
                pool.wait_ge(d_plan, n + 1)
                pool.wait_ge(e_T, n * NB)
                step_past(pool, pool_past)
                for k in range(2):
                    for i in range(TW):
                        pool.indirect_dma_start(
                            out=sorted_in[p], out_offset=bass.IndirectOffsetOnAxis(ap=idx[:, p, k, i:i + 1], axis=0),
                            in_=xn[:, p, i, :], in_offset=None).then_inc(scattered[p], 16)

            def gather(n, p):
                for s in range(RING):
                    pool.wait_ge(y_stored[s], 16 * PER_SLOT * (n + 1))
                pool.wait_ge(c_x, TW * n)
                step_past(pool, pool_past)
                for k in range(2):
                    for i in range(TW):
                        pool.indirect_dma_start(
                            out=yg[:, k, i, :], out_offset=None, in_=sorted_out[p],
                            in_offset=bass.IndirectOffsetOnAxis(ap=idx[:, p, k, i:i + 1], axis=0)).then_inc(gathered, 16)

            with pool.Fori(0, NW) as w:
                for p in range(2):
                    scatter(2 * w + p, w, p)
                    gather(2 * w + p, p)

        @block.scalar
        def _(act):
            act.wait_ge(weights_loaded, 16 * WEIGHT_DMAS)
            act.activation(aneg_sb[:], aneg_sb[:], ACT.Exp).then_inc(fixed_act, 1)
            consts_ready(act)

            def dispatch(n):
                for half in range(2):
                    act.wait_ge(d_T, 2 * n + half + 1)
                    act.wait_ge(d_logits, n)
                    act.activation(xnT[:, 512 * half:512 * half + 512], bank[6][:], ACT.Copy).then_inc(d_xT, 1)
                act.wait_ge(d_margin, n + 1)
                act.activation(ex[:], dm[:], ACT.Exp).then_inc(d_exp, 1)

            def expert(n):
                def take_x(r, u):
                    b = r * RING + u
                    act.wait_ge(e_T, n * NB + b + 1)
                    act.wait_ge(e_H, n * NB + (b - 1 if u >= 2 else 0))
                    act.activation(xbT[:, u % 2, :], bank[u % 2][:, 0:P], ACT.Copy).then_inc(e_xT, 1)

                for u in range(RING):
                    take_x(0, u)
                with act.Fori(0, ROUNDS) as r:
                    for s in range(RING):
                        take_x(r, s + RING)

            def mix0(w):
                for half in range(2):
                    act.wait_ge(m_T, 2 * w + half + 1)
                    act.activation(unT[:, 512 * half:512 * half + 512], bank[6][:], ACT.Identity,
                                   bias=lnb_sb[:], scale=lng_sb[:]).then_inc(m_uT, 1)
                act.wait_ge(m_abs, w + 1)
                act.activation(dte[:], dta[:], ACT.Exp, scale=-1.0).then_inc(m_exp, 1)
                act.wait_ge(m_one, w + 1)
                act.activation(dtl[:], dtu[:], ACT.Ln).then_inc(m_log, 1)
                act.wait_ge(m_csT, w + 1)
                act.activation(cs_r[:], bank[7][0:CH * BW * NHEADS, 0:P], ACT.Copy).then_inc(m_csr, 1)

            def project(w):
                ch = Chain(act, p_chain, 0)
                for q in range(2):
                    for i in range(4):
                        k = 4 * q + i
                        act.wait_ge(p_xbc, 8 * w + k + 1)
                        if k >= 2:
                            act.wait_ge(p_silu, 8 * w + k - 1)
                        act.activation(acc[:, k % 2, :], bank[k % 4][:], ACT.Identity, bias=conv_b_sb[:, i:i + 1],
                                       scale=conv_w_sb[:, i, D_CONV - 1:D_CONV]).then_inc(p_acc, 1)
                        if k >= 1:
                            silu(w, k - 1)
                    if q == 1:
                        silu(w, 7)
                    for m in range(2):
                        act.wait_ge(p_z, 4 * w + 2 * q + m + 1)
                        act.activation(zs[:, m, 512 * q:512 * q + 512], bank[4 + m][:], ACT.Silu).then_inc(p_zs, 1)

            def silu(w, k):
                act.wait_ge(p_tap, 8 * w + k + 1)
                act.activation(xbc[:, k % 4, 512 * (k // 4):512 * (k // 4) + 512], acc[:, k % 2, :],
                               ACT.Silu).then_inc(p_silu, 1)

            def scan(w):
                def decays(j):
                    if j == 0:
                        act.wait_ge(cs_loaded, 16 * (w + 1))
                    act.wait_ge(b_mix, 2 * BW * w + 2 * max(j - 1, 0))
                    first, second = decay_view(decay[:, j % 2, :])
                    for h in range(NHEADS):
                        act.activation(first[:, h, :].rearrange("p (c l) -> p c l", c=CH),
                                       csb[:, :, j * NHEADS + h, :], ACT.Exp,
                                       bias=ncs_t[:, 0, j, h:h + 1]).then_inc(b_decay, 1)
                    for h in range(NHEADS):
                        act.activation(second[:, h, :], csb[:, 1, j * NHEADS + h, :], ACT.Exp,
                                       bias=ncs_t[:, 1, j, h:h + 1]).then_inc(b_decay, 1)

                def square(j):
                    act.wait_ge(b_yz, BW * w + j + 1)
                    act.wait_ge(b_ss, BW * w + max(j - 1, 0))
                    act.activation(sq[:, j % 2], yz[:, j % 2], ACT.Square).then_inc(b_sq, 1)

                decays(0)
                for j in range(BW):
                    if j + 1 < BW:
                        decays(j + 1)
                    square(j)

            with act.Fori(0, NW) as w:
                dispatch(2 * w)
                expert(2 * w)
                mix0(w)
                project(w)
                scan(w)
                dispatch(2 * w + 1)
                expert(2 * w + 1)

        @block.tensor
        def _(pe):
            consts_ready(pe)

            def turn(dst, src, sem_after=None):
                ins = pe.transpose(dst, src, ident[:])
                return ins

            def dispatch(n, p):
                for half in range(2):
                    if half == 0:
                        pe.wait_ge(d_plan, n)
                    else:
                        pe.wait_ge(d_xT, 2 * n + 1)
                    pe.wait_ge(d_xn, TW * n + 4 * half + 4)
                    for i in range(4):
                        mm = pe.transpose(bank[6][:, P * i:P * i + P], xn[:, p, 4 * half + i, :], ident[:])
                    mm.then_inc(d_T, 1)
                for half in range(2):
                    pe.wait_ge(d_xT, 2 * n + half + 1)
                    for i in range(4 * half, 4 * half + 4):
                        mm = pe.matmul(bank[7][:, 64 * i:64 * i + 64], xnT[:, P * i:P * i + P], wr_pad[:],
                                       start=True, stop=True)
                mm.then_inc(d_logits, 1)
                pe.wait_ge(d_chosen, n + 1)
                by_expert = chosen[:].rearrange("p i e -> p e i")
                pe.matmul(bank[6][:, 0:64], below_bf[:], by_expert, start=True, stop=True)
                pe.matmul(bank[6][:, 64:128], ones_bf[:], by_expert, start=True, stop=True).then_inc(d_rank, 1)

            def expert(n, p):
                pe.wait_ge(d_plan, n + 1)

                def turn_x(r, u):
                    b = r * RING + u
                    pe.wait_ge(xb_loaded[u % RING], 16 * (PER_SLOT * n + r + u // RING + 1))
                    pe.wait_ge(e_xT, n * NB + (b - 1 if u >= 2 else 0))
                    pe.transpose(bank[u % 2][:, 0:P], xb[:, u % RING, :], ident[:]).then_inc(e_T, 1)

                def up(r, u):
                    b = r * RING + u
                    pe.wait_ge(w1_loaded[u % RING], 16 * (PER_SLOT * n + r + u // RING + 1))
                    pe.wait_ge(e_xT, n * NB + b + 1)
                    pe.wait_ge(e_h, n * NB + (b - 1 if u >= 2 else 0))
                    for f in range(2):
                        mm = pe.matmul(bank[2 + u % 2][:, P * f:P * f + P], w1b[:, u % RING, P * f:P * f + P],
                                       xbT[:, u % 2, :], start=True, stop=True)
                    mm.then_inc(e_H, 1)

                def down(r, u):
                    b = r * RING + u
                    e = pe.value_load(block_expert[0:1, p, bass.ds(b, 1)], min_val=0, max_val=NEXP - 1)
                    pe.wait_ge(e_h, n * NB + b + 1)
                    pe.wait_ge(e_y, n * NB + (b - 1 if u >= 2 else 0))
                    for f in range(2):
                        mm = pe.matmul(bank[4 + u % 2][:, 0:P], hb[:, u % 2, f, :],
                                       w2_sb[:, bass.ds(2 * e + f, 1), :].rearrange("p a d -> p (a d)"),
                                       start=(f == 0), stop=(f == 1))
                    mm.then_inc(e_Y, 1)

                turn_x(0, 0)
                turn_x(0, 1)
                up(0, 0)
                for u in range(RING):
                    turn_x(0, u + 2)
                    up(0, u + 1)
                    down(0, u)
                with pe.Fori(0, ROUNDS - 1) as r:
                    for u in range(RING, 2 * RING):
                        turn_x(r, u + 2)
                        up(r, u + 1)
                        down(r, u)
                for b in range(TAIL, NB):
                    if b + 2 < NB:
                        turn_x(0, b + 2)
                    if b + 1 < NB:
                        up(0, b + 1)
                    down(0, b)

            def mix0(w):
                for half in range(2):
                    pe.wait_ge(m_u, TW * w + 4 * half + 4)
                    if half == 1:
                        pe.wait_ge(m_uT, 2 * w + 1)
                    for i in range(4):
                        mm = pe.transpose(bank[6][:, P * i:P * i + P], un[:, 4 * half + i, :], ident[:])
                    mm.then_inc(m_T, 1)
                pe.wait_ge(m_uT, 2 * w + 2)
                for i in range(TW):
                    mm = pe.matmul(bank[7][:, 64 * i:64 * i + 64], unT[:, P * i:P * i + P],
                                   w_in_sb[:, NPROJ - 64:NPROJ], start=True, stop=True)
                mm.then_inc(m_dt, 1)
                pe.wait_ge(m_a, w + 1)
                half = BW * NHEADS
                a_rows = a_t[:].rearrange("p c j h -> p (c j h)")
                pe.matmul(bank[6][:, 0:2 * half], upper[:], a_rows, start=True, stop=False)
                pe.matmul(bank[6][:, half:2 * half], ones[:], a_rows[:, 0:half], start=False,
                          stop=True).then_inc(m_cs, 1)
                pe.wait_ge(m_cst, w + 1)
                pe.transpose(bank[7][0:2 * half, 0:P], cs_t[:], ident[:]).then_inc(m_csT, 1)

            def project(w):
                for q in range(2):
                    for i in range(4):
                        k = 4 * q + i
                        pe.wait_ge(p_tap, 8 * w + max(k - 3, 0))
                        pe.matmul(bank[k % 4][:], w_in_sb[:, XCOL + P * i:XCOL + P * i + P],
                                  unT[:, 512 * q:512 * q + 512], start=True, stop=True).then_inc(p_xbc, 1)
                    for m in range(2):
                        pe.wait_ge(p_zs, 4 * w + 2 * q)
                        pe.matmul(bank[4 + m][:], w_in_sb[:, ZCOL + P * m:ZCOL + P * m + P],
                                  unT[:, 512 * q:512 * q + 512], start=True, stop=True).then_inc(p_z, 1)

            def scan(w):
                def sources(j):
                    pe.wait_ge(b_xdt, BW * w + j)
                    for c in range(CH):
                        for m in range(2):
                            t = SEQ * j + P * c
                            mm = pe.transpose(bank[0][:, 256 * c + P * m:256 * c + P * m + P],
                                              xbc[:, m, t:t + P], ident[:])
                    mm.then_inc(b_T, 1)
                    pe.wait_ge(b_gm, BW * w + j)
                    t = SEQ * j
                    pe.matmul(bank[1][:, 0:SEQ], xbc[:, 2, t:t + P], xbc[:, 3, t:t + SEQ], start=True, stop=True)
                    pe.matmul(bank[1][:, SEQ:SEQ + P], xbc[:, 2, t + P:t + SEQ], xbc[:, 3, t + P:t + SEQ],
                              start=True, stop=True).then_inc(b_G, 1)

                def outputs(j):
                    pe.wait_ge(b_mix, 2 * (BW * w + j + 1))
                    pe.wait_ge(b_xdt, BW * w + j + 1)
                    pe.wait_ge(b_yz, BW * w + max(j - 1, 0))
                    first, second = decay_view(mix[:, j % 2, :])
                    for h in range(NHEADS):
                        a = HEADDIM * (h % 2)
                        o = bank[2 + j % 2][a:a + HEADDIM, SEQ * (h // 2):SEQ * (h // 2) + SEQ]
                        pe.matmul(o, xdt[:, j % 2, 0, h, :], first[:, h, :], start=True, stop=False)
                        mm = pe.matmul(o[:, P:SEQ], xdt[:, j % 2, 1, h, :], second[:, h, :], start=False, stop=True)
                    mm.then_inc(b_Y, 1)

                def out_rows_of(j):
                    pe.wait_ge(b_ss, BW * w + j + 1)
                    for c in range(CH):
                        i = CH * j + c
                        o = bank[4 + i // 4][:, P * (i % 4):P * (i % 4) + P]
                        for m in range(2):
                            pe.matmul(o, yz[:, j % 2, m, P * c:P * c + P], w_out_sb[:, m, :],
                                      start=(m == 0), stop=(m == 1))
                        mm = pe.matmul(bank[6][:, 64 * i:64 * i + 64], ss[:, j % 2, P * c:P * c + P],
                                       ones[:, 0:64], start=True, stop=True)
                    mm.then_inc(b_O, 1)

                pe.wait_ge(p_silu, 8 * (w + 1))
                sources(0)
                sources(1)
                outputs(0)
                for j in range(BW):
                    if j + 2 < BW:
                        sources(j + 2)
                    if j + 1 < BW:
                        outputs(j + 1)
                    out_rows_of(j)

            with pe.Fori(0, NW) as w:
                dispatch(2 * w, 0)
                expert(2 * w, 0)
                mix0(w)
                project(w)
                scan(w)
                dispatch(2 * w + 1, 1)
                expert(2 * w + 1, 1)

        @block.vector
        def _(dve):
            dve.wait_ge(weights_loaded, 16 * WEIGHT_DMAS)
            dve.wait_ge(fixed_act, 1)
            dve.tensor_scalar(aneg_sb[:], aneg_sb[:], -1.0, None, ALU.mult).then_inc(fixed_dve, 1)
            for m in range(2):
                dve.tensor_scalar(w_out_sb[:, m, :], w_out_sb[:, m, :], normw_sb[:, m:m + 1], None,
                                  ALU.mult).then_inc(fixed_dve, 1)
            dve.sem_inc(fixed_dve, 4)
            consts_ready(dve)

            def rsqrt(ch, v):
                y = rs_y[:].bitcast(F32)
                ch.link(dve.tensor_scalar(rs_i[:], v.bitcast(I32), 1, None, ALU.logical_shift_right))
                ch.link(dve.tensor_scalar(rs_y[:], rs_i[:], -1.0, float(MAGIC), ALU.mult, ALU.add))
                ch.link(dve.tensor_scalar(rs_h[:], v, -0.5, None, ALU.mult))
                for _ in range(3):
                    ch.link(dve.tensor_tensor(rs_t[:], y, y, ALU.mult))
                    ch.link(dve.tensor_tensor(rs_t[:], rs_t[:], rs_h[:], ALU.mult))
                    ch.link(dve.scalar_tensor_tensor(y, rs_t[:], 1.5, y, ALU.add, ALU.mult))
                return y

            def moments(ch, w):
                step_past(dve, dve_past)
                for i in range(TW):
                    ch.mark(dve.bn_stats(stats[:, i, :], X[:, bass.ds(w * TW + i, 1), :].rearrange("p a d -> p (a d)")))
                ch.settle()
                step_past(dve, dve_past)
                for i in range(TW):
                    ch.mark(dve.bn_aggr(mv[:, i, :], stats[:, i, :]))
                ch.settle()
                ch.link(dve.tensor_scalar(rs_v[:], mv[:, :, 1], EPS, None, ALU.add))

            def x_tile(w, i):
                return X[:, bass.ds(w * TW + i, 1), :].rearrange("p a d -> p (a d)")

            def over_experts(a):
                return a.unsqueeze(2).broadcast_to([P, TW, NEXP])

            def dispatch(n, w, p):
                ch = Chain(dve, d_chain, n * DISPATCH_STEPS)
                moments(ch, w)
                y = rsqrt(ch, rs_v[:])
                dve.wait_ge(scattered[p], 256 * w)
                for i in range(TW):
                    dve.tensor_scalar(xn[:, p, i, :], x_tile(w, i), mv[:, i, 0:1], y[:, i:i + 1],
                                      ALU.subtract, ALU.mult).then_inc(d_xn, 1)
                dve.wait_ge(d_logits, n + 1)
                logits = bank[7][:].rearrange("p (i e) -> p i e", i=TW)[:, :, 0:NEXP]
                ch.link(dve.tensor_tensor(lg[:], logits, br_sb[:].unsqueeze(1).broadcast_to([P, TW, NEXP]), ALU.add))
                src = lg
                for k in range(2):
                    ch.link(dve.tensor_reduce(mx[:, 2 * k, :], src[:], AX.X, ALU.max))
                    ch.link(dve.tensor_tensor(sc[:], src[:], over_experts(mx[:, 2 * k, :]), ALU.is_equal))
                    ch.link(dve.tensor_tensor(sc[:], sc[:], expert_rev[:], ALU.mult))
                    ch.link(dve.tensor_reduce(mx[:, 2 * k + 1, :], sc[:], AX.X, ALU.max))
                    ch.link(dve.tensor_tensor(oh[:, k], expert_rev[:], over_experts(mx[:, 2 * k + 1, :]), ALU.is_equal))
                    if k == 0:
                        ch.link(dve.scalar_tensor_tensor(lg2[:], oh[:, 0], -HUGE, lg[:], ALU.mult, ALU.add))
                        src = lg2
                dve.tensor_tensor(chosen[:], oh[:, 0], oh[:, 1], ALU.add).then_inc(d_chosen, 1)
                dve.tensor_tensor(dm[:], mx[:, 2, :], mx[:, 0, :], ALU.subtract).then_inc(d_margin, 1)
                dve.wait_ge(d_exp, n + 1)
                ch.link(dve.tensor_scalar(rs_t[:], ex[:], 2.0, 2.0, ALU.mult, ALU.add))
                ch.link(dve.reciprocal(gate[:, p, 0, :], rs_t[:]))
                ch.mark(dve.tensor_tensor(gate[:, p, 1, :], gate[:, p, 0, :], ex[:], ALU.mult))
                dve.wait_ge(d_rank, n + 1)
                before = bank[6][:, 0:64].rearrange("p (e i) -> p e i", e=NEXP)
                total = bank[6][:, 64:128].rearrange("p (e i) -> p e i", e=NEXP)
                ch.link(dve.tensor_tensor_scan(incl[:].rearrange("p e i -> p (e i)"),
                                               not_first[:].rearrange("p e i -> p (e i)"), bank[6][:, 64:128],
                                               0.0, ALU.mult, ALU.add))
                ch.link(dve.tensor_tensor(rank[:], incl[:], total, ALU.subtract))
                ch.link(dve.tensor_tensor(rank[:], rank[:], before, ALU.add))
                ch.link(dve.tensor_tensor(cmp[:], incl[:, :, TW - 1:TW].broadcast_to([P, NEXP, TW]), tile_start[:],
                                          ALU.is_gt))
                ch.link(dve.tensor_reduce(nblk[:], cmp[:], AX.X, ALU.add))
                ch.link(dve.tensor_tensor_scan(bend[:], ones[:, 0:NEXP], nblk[:], 0.0, ALU.mult, ALU.add))
                ch.link(dve.tensor_tensor(bstart[:], bend[:], nblk[:], ALU.subtract))
                ch.link(dve.scalar_tensor_tensor(rank[:], bstart[:].unsqueeze(2).broadcast_to([P, NEXP, TW]), float(P),
                                                 rank[:], ALU.mult, ALU.add))
                by_tile = rank[:].rearrange("p e i -> p i e")
                for k in range(2):
                    ch.link(dve.tensor_tensor(sc[:], oh[:, k], by_tile, ALU.mult))
                    ch.link(dve.tensor_reduce(pos[:, k, :], sc[:], AX.X, ALU.add))
                ch.link(dve.tensor_tensor(bcmp[:], bend[0:1, :].unsqueeze(1).broadcast_to([1, NB, NEXP]), block_no[:],
                                          ALU.is_le))
                ch.link(dve.tensor_reduce(bsum[:], bcmp[:], AX.X, ALU.add))
                ch.mark(dve.tensor_scalar(block_expert[0:1, p, :], bsum[:], float(NEXP - 1), None, ALU.min))
                assert ch.k == DISPATCH_STEPS, ch.k
                dve.tensor_copy(idx[:, p], pos[:]).then_inc(d_plan, 1)

            def expert(n, p):
                def hidden(r, u):
                    b = r * RING + u
                    dve.wait_ge(e_H, n * NB + b + 1)
                    dve.wait_ge(e_Y, n * NB + (b - 1 if u >= 2 else 0))
                    for f in range(2):
                        ins = dve.tensor_scalar(hb[:, u % 2, f, :], bank[2 + u % 2][:, P * f:P * f + P],
                                                w1b[:, u % RING, FF + f:FF + f + 1], 0.0, ALU.add, ALU.max)
                    ins.then_inc(e_h, 1)

                def rows(r, u):
                    b = r * RING + u
                    e = dve.value_load(block_expert[0:1, p, bass.ds(b, 1)], min_val=0, max_val=NEXP - 1)
                    dve.wait_ge(e_Y, n * NB + b + 1)
                    dve.wait_ge(y_stored[u % RING], 16 * (PER_SLOT * n + r + u // RING))
                    dve.tensor_tensor(yb[:, u % RING, :].unsqueeze(1), bank[4 + u % 2][:, 0:P].unsqueeze(1),
                                      b2_sb[:, bass.ds(e, 1), :], ALU.add).then_inc(e_y, 1)

                dve.wait_ge(d_plan, n + 1)
                hidden(0, 0)
                for u in range(RING):
                    hidden(0, u + 1)
                    rows(0, u)
                with dve.Fori(0, ROUNDS - 1) as r:
                    for u in range(RING, 2 * RING):
                        hidden(r, u + 1)
                        rows(r, u)
                for b in range(TAIL, NB):
                    if b + 1 < NB:
                        hidden(0, b + 1)
                    rows(0, b)

            def combine(n, w, p):
                ch = Chain(dve, c_chain, n * COMBINE_STEPS)
                dve.wait_ge(gathered, 256 * (n + 1))
                for i in range(TW):
                    ch.mark(dve.scalar_tensor_tensor(x_tile(w, i), yg[:, 0, i, :], gate[:, p, 0, i:i + 1],
                                                     x_tile(w, i), ALU.mult, ALU.add))
                ch.settle()
                for i in range(TW):
                    dve.scalar_tensor_tensor(x_tile(w, i), yg[:, 1, i, :], gate[:, p, 1, i:i + 1],
                                             x_tile(w, i), ALU.mult, ALU.add).then_inc(c_x, 1)
                dve.wait_ge(c_x, TW * (n + 1))
                assert ch.k == COMBINE_STEPS

            def mix0(w):
                ch = Chain(dve, m_chain, w * MIX0_STEPS)
                moments(ch, w)
                y = rsqrt(ch, rs_v[:])
                ch.link(dve.tensor_copy(r1[:], y))
                ch.link(dve.tensor_tensor(rs_t[:], r1[:], r1[:], ALU.mult))
                ch.link(dve.tensor_tensor(rs_v[:], rs_t[:], mv[:, :, 1], ALU.mult))
                ch.link(dve.tensor_scalar(rs_v[:], rs_v[:], EPS, None, ALU.add))
                y = rsqrt(ch, rs_v[:])
                ch.link(dve.tensor_tensor(rs_h[:], r1[:], y, ALU.mult))
                for i in range(TW):
                    dve.tensor_scalar(un[:, i, :], x_tile(w, i), mv[:, i, 0:1], rs_h[:, i:i + 1],
                                      ALU.subtract, ALU.mult).then_inc(m_u, 1)
                ch.link(dve.scalar_tensor_tensor(rs_t[:], mv[:, :, 0], -1.0, r1[:], ALU.mult, ALU.mult))
                ch.link(dve.tensor_scalar(rs_v[:], r1[:], 1.0, None, ALU.add))
                dve.wait_ge(m_u, TW * (w + 1))
                for i in range(TW):
                    ch.mark(dve.tensor_scalar(x_tile(w, i), x_tile(w, i), rs_v[:, i:i + 1], rs_t[:, i:i + 1],
                                              ALU.mult, ALU.add))
                dve.wait_ge(m_dt, w + 1)
                raw = bank[7][:].rearrange("p (j c f) -> p c j f", j=BW, c=CH)[:, :, :, 64 - NHEADS:64]
                for c in range(CH):
                    ch.mark(dve.tensor_tensor(dtx[:, c], raw[:, c], dtb_sb[:].unsqueeze(1).broadcast_to([P, BW, NHEADS]),
                                              ALU.add))
                ch.settle()
                dve.scalar_tensor_tensor(dta[:], dtx[:], -1.0, dtx[:], ALU.mult, ALU.max).then_inc(m_abs, 1)
                dve.wait_ge(m_exp, w + 1)
                dve.tensor_scalar(dtu[:], dte[:], 1.0, None, ALU.add).then_inc(m_one, 1)
                dve.wait_ge(m_one, w + 1)
                ch.mark(dve.reciprocal(dtr[:], dtu[:]))
                ch.link(dve.tensor_scalar(dta[:], dtu[:], -1.0, None, ALU.add))
                ch.link(dve.scalar_tensor_tensor(dta[:], dta[:], -1.0, dte[:], ALU.mult, ALU.add))
                ch.link(dve.tensor_tensor(dta[:], dta[:], dtr[:], ALU.mult))
                dve.wait_ge(m_log, w + 1)
                ch.link(dve.tensor_tensor(dta[:], dta[:], dtl[:], ALU.add))
                ch.link(dve.scalar_tensor_tensor(dt_t[:], dtx[:], 0.0, dta[:], ALU.max, ALU.add))
                dve.tensor_tensor(a_t[:].rearrange("p c j h -> p (c j) h"), dt_t[:].rearrange("p c j h -> p (c j) h"),
                                  aneg_sb[:].unsqueeze(1).broadcast_to([P, CH * BW, NHEADS]), ALU.mult).then_inc(m_a, 1)
                dve.wait_ge(m_cs, w + 1)
                dve.wait_ge(b_decay, 8 * BW * w)
                sums = bank[6][:, 0:CH * BW * NHEADS]
                dve.tensor_copy(cs_t[:], sums).then_inc(m_cst, 1)
                ch.link(dve.tensor_scalar(ncs_t[:].rearrange("p c j h -> p (c j h)"), sums, -1.0, None, ALU.mult))
                assert ch.k == MIX0_STEPS, ch.k

            def project(w):
                for q in range(2):
                    for i in range(4):
                        k = 4 * q + i
                        dve.wait_ge(p_acc, 8 * w + k + 1)
                        a = acc[:, k % 2, :].rearrange("p (j t) -> p j t", j=2)
                        v = bank[k % 4][:].rearrange("p (j t) -> p j t", j=2)
                        for back in range(1, D_CONV):
                            if back > 1:
                                dve.wait_ge(b_chain, 16 * w + 2 * k + back - 1)
                            ins = dve.scalar_tensor_tensor(
                                a[:, :, back:], v[:, :, :SEQ - back], conv_w_sb[:, i, D_CONV - 1 - back:D_CONV - back],
                                a[:, :, back:], ALU.mult, ALU.add)
                            ins.then_inc(b_chain if back < D_CONV - 1 else p_tap, 1)

            def scan(w):
                def weights(j):
                    dve.wait_ge(b_T, BW * w + j + 1)
                    dve.wait_ge(b_Y, BW * w + max(j - 1, 0))
                    dve.tensor_tensor(xdt[:, j % 2].rearrange("p c h d -> p c (h d)").rearrange("p c (h d) -> p c h d", h=NHEADS),
                                      bank[0][:].rearrange("p (c h d) -> p c h d", c=CH, h=NHEADS),
                                      dt_t[:, :, j, :].unsqueeze(3).broadcast_to([P, CH, NHEADS, HEADDIM]),
                                      ALU.mult).then_inc(b_xdt, 1)
                    dve.wait_ge(b_G, BW * w + j + 1)
                    dve.tensor_tensor(gm[:, j % 2].rearrange("p a l -> p (a l)"), bank[1][:, 0:3 * P],
                                      causal[:].rearrange("p a l -> p (a l)"), ALU.mult).then_inc(b_gm, 1)
                    dve.wait_ge(b_gm, BW * w + j + 1)
                    dve.wait_ge(b_decay, 8 * (BW * w + j + 1))
                    dec, mixed = decay_view(decay[:, j % 2, :]), decay_view(mix[:, j % 2, :])
                    g = gm[:, j % 2].rearrange("p a l -> p (a l)")
                    for part, cols in ((0, slice(0, SEQ)), (1, slice(SEQ, 3 * P))):
                        n = cols.stop - cols.start
                        dve.scalar_tensor_tensor(mixed[part], dec[part], 1.0,
                                                 g[:, cols].unsqueeze(1).broadcast_to([P, NHEADS, n]),
                                                 ALU.min, ALU.mult).then_inc(b_mix, 1)

                def gated(j, ch):
                    dve.wait_ge(b_Y, BW * w + j + 1)
                    dve.wait_ge(b_O, BW * w + max(j - 1, 0))
                    for m in range(2):
                        t = slice(SEQ * j, SEQ * j + SEQ)
                        ch.mark(dve.scalar_tensor_tensor(yz[:, j % 2, m, :], xbc[:, m, t], dskip_sb[:, m:m + 1],
                                                         bank[2 + j % 2][:, SEQ * m:SEQ * m + SEQ], ALU.mult, ALU.add))
                    ch.settle()
                    dve.tensor_tensor(yz[:, j % 2], yz[:, j % 2], zs[:, :, SEQ * j:SEQ * j + SEQ],
                                      ALU.mult).then_inc(b_yz, 1)

                def squares(j, ch):
                    dve.wait_ge(b_sq, BW * w + j + 1)
                    dve.tensor_tensor(ss[:, j % 2, :], sq[:, j % 2, 0, :], sq[:, j % 2, 1, :],
                                      ALU.add).then_inc(b_ss, 1)

                ch = Chain(dve, c2_chain, w * MIX1_STEPS)
                dve.wait_ge(p_zs, 4 * (w + 1))
                weights(0)
                for j in range(BW):
                    if j + 1 < BW:
                        weights(j + 1)
                    gated(j, ch)
                    squares(j, ch)
                dve.wait_ge(b_O, BW * (w + 1))
                sums = bank[6][:].rearrange("p (i e) -> p i e", i=TW)[:, :, 0]
                ch.link(dve.tensor_scalar(rs_v[:], sums, 1.0 / D_INNER, EPS, ALU.mult, ALU.add))
                y = rsqrt(ch, rs_v[:])
                for i in range(TW):
                    dve.scalar_tensor_tensor(x_tile(w, i), bank[4 + i // 4][:, P * (i % 4):P * (i % 4) + P],
                                             y[:, i:i + 1], x_tile(w, i), ALU.mult, ALU.add).then_inc(b_x, 1)
                dve.wait_ge(b_x, TW * (w + 1))
                assert ch.k == MIX1_STEPS, ch.k

            with dve.Fori(0, NW) as w:
                dve.wait_ge(x_loaded, 16 * (w + 1))
                dispatch(2 * w, w, 0)
                expert(2 * w, 0)
                combine(2 * w, w, 0)
                mix0(w)
                project(w)
                scan(w)
                dispatch(2 * w + 1, w, 1)
                expert(2 * w + 1, 1)
                combine(2 * w + 1, w, 1)


def kernel(**inputs):
    import numpy as np
    import concourse.bacc as bacc
    from concourse.bass_utils import run_bass_kernel_spmd

    def col(v, m):
        v = np.asarray(v)
        return np.ascontiguousarray(np.moveaxis(v.reshape(m, P, *v.shape[1:]), 0, 1))

    a = {k.removeprefix("L0_"): np.asarray(v) for k, v in inputs.items()}
    arrays = {
        "x": a["attn_x"], "w_in_t": np.ascontiguousarray(a["attn_W_in"].T),
        "conv_w": col(a["attn_conv_w"], 4), "conv_b": col(a["attn_conv_b"], 4),
        "dt_bias": a["attn_dt_bias"], "a_log": a["attn_A_log"], "dskip": np.ascontiguousarray(a["attn_Dskip"].reshape(2, 2).T),
        "norm_w": col(a["attn_norm_w"], 2), "w_out_t": np.ascontiguousarray(a["attn_W_out"].T),
        "ln_g": a["attn_ln_g"].reshape(P, 1), "ln_b": a["attn_ln_b"].reshape(P, 1),
        "wr": a["ffn_Wr"], "br": a["ffn_br"], "w1": a["ffn_W1"],
        "b1": np.ascontiguousarray(a["ffn_b1"].reshape(NEXP, 2, P).transpose(2, 0, 1)),
        "w2": a["ffn_W2"], "b2": a["ffn_b2"],
    }
    nc = bacc.Bacc("TRN2", target_bir_lowering=False, num_devices=1)
    args = {n: nc.dram_tensor(f"in_{n}", v.shape, mybir.dt.from_np(v.dtype), kind="ExternalInput").ap()
            for n, v in arrays.items()}
    out = nc.dram_tensor("out", a["attn_x"].shape, F32, kind="ExternalOutput").ap()
    build_program(nc, out=out, **args)
    result = run_bass_kernel_spmd(nc, [{f"in_{n}": v for n, v in arrays.items()}], core_ids=[0])
    return result.results[0]["out"]
```

```python
from contextlib import ExitStack

import concourse.bass as bass
from concourse import mybir

ALU = mybir.AluOpType
ACT = mybir.ActivationFunctionType
AX = mybir.AxisListType
F32 = mybir.dt.float32
BF16 = mybir.dt.bfloat16
I32 = mybir.dt.int32

P = 128
D = 128
D_INNER = 256
NHEADS = 4
HEADDIM = D_INNER // NHEADS
NSTATE = 128
D_CONV = 4
NEXP = 8
FF = 256
EPS = 1e-5

SEQ = 256
CH = SEQ // P
BW = 4
TW = BW * CH
ROWS_BOUND = (2 * TW * P + NEXP * (P - 1)) // P
PAIRS = 4
RING = 2 * PAIRS
NB = -(-ROWS_BOUND // RING) * RING
ROUNDS = NB // RING
ZCOL, XCOL, DTCOL = 0, D_INNER, 2 * D_INNER + 2 * NSTATE
NPROJ = DTCOL + NHEADS
MAGIC = 0x5F3759DF
HUGE = 3.0e38


class Chain:

    def __init__(self, eng, sem, base):
        self.eng, self.sem, self.base, self.k = eng, sem, base, 0

    def mark(self, ins):
        ins.then_inc(self.sem, 1)
        self.k += 1

    def settle(self):
        self.eng.wait_ge(self.sem, self.base + self.k)

    def link(self, ins):
        self.mark(ins)
        yield
        self.settle()


def advance(side, pieces=1):
    for _ in range(pieces):
        next(side, None)


def finish(side):
    for _ in side:
        pass


RSQRT_STEPS = 12
DISPATCH_STEPS = 2 * TW + 1 + RSQRT_STEPS + 30
MIX0_STEPS = 3 * TW + 2 * RSQRT_STEPS + 17
SCAN_STEPS = 2 * BW + 1 + RSQRT_STEPS
COMBINE_STEPS = TW


def build_program(nc, x, w_in_t, conv_w, conv_b, dt_bias, a_log, dskip, norm_w, w_out_t,
                  ln_g, ln_b, wr, br, w1, b1, w2, b2, out):
    n_seq = x.shape[0]
    NT = n_seq * SEQ // P
    NW = NT // TW
    assert NT == NW * TW and NW > 4

    x_rows = x.rearrange("b (c p) d -> p (b c) d", p=P)
    out_rows = out.rearrange("b (c p) d -> p (b c) d", p=P)
    sorted_in = [nc.dram_tensor(f"sorted_in{p}", [NB * P, D], F32, kind="Internal").ap() for p in range(2)]
    sorted_out = [nc.dram_tensor(f"sorted_out{p}", [NB * P, D], F32, kind="Internal").ap() for p in range(2)]
    cs_dram = nc.dram_tensor("cs_rows", [CH * BW * NHEADS, P], F32, kind="Internal").ap()

    with ExitStack() as ctx:
        def sb(name, shape, dt=F32):
            return ctx.enter_context(nc.sbuf_tensor(name, shape, dt))

        def sem(name):
            return ctx.enter_context(nc.semaphore(name))

        ident = sb("ident", [P, P])
        upper = sb("upper", [P, P])
        below_bf = sb("below_bf", [P, P], BF16)
        ones = sb("ones", [P, P])
        ones_bf = sb("ones_bf", [P, P], BF16)
        causal = sb("causal", [P, 3, P])
        expert_rev = sb("expert_rev", [P, TW, NEXP])
        tile_start = sb("tile_start", [P, NEXP, TW])
        block_no = sb("block_no", [1, NB, NEXP])
        not_first = sb("not_first", [P, NEXP, TW])
        itmp = sb("itmp", [P, NB * NEXP], I32)
        w_in_sb = sb("w_in_sb", [P, NPROJ])
        w_out_sb = sb("w_out_sb", [P, 2, D])
        conv_w_sb = sb("conv_w_sb", [P, 4, D_CONV])
        conv_b_sb = sb("conv_b_sb", [P, 4])
        dtb_sb = sb("dtb_sb", [P, NHEADS])
        aneg_sb = sb("aneg_sb", [P, NHEADS])
        dskip_sb = sb("dskip_sb", [P, 2])
        normw_sb = sb("normw_sb", [P, 2])
        lng_sb = sb("lng_sb", [P, 1])
        lnb_sb = sb("lnb_sb", [P, 1])
        wr_pad = sb("wr_pad", [P, 64])
        br_sb = sb("br_sb", [P, NEXP])
        w1_sb = sb("w1_sb", [P, NEXP, FF + 2])
        w2_sb = sb("w2_sb", [P, 2 * NEXP, D])
        b2_sb = sb("b2_sb", [P, NEXP, D])

        X = sb("X", [P, NT, D])
        stats = sb("stats", [P, TW, 6])
        mv = sb("mv", [P, TW, 2])
        rs_v = sb("rs_v", [P, TW])
        rs_i = sb("rs_i", [P, TW], I32)
        rs_h = sb("rs_h", [P, TW])
        rs_t = sb("rs_t", [P, TW])
        rs_y = sb("rs_y", [P, TW], I32)
        fin_v = sb("fin_v", [P, TW])
        fin_i = sb("fin_i", [P, TW], I32)
        fin_h = sb("fin_h", [P, TW])
        fin_t = sb("fin_t", [P, TW])
        fin_y = sb("fin_y", [P, TW], I32)
        xn = sb("xn", [P, 2, TW, D])
        xnT = sb("xnT", [P, TW * P])
        lg = sb("lg", [P, TW, NEXP])
        lg2 = sb("lg2", [P, TW, NEXP])
        sc = sb("sc", [P, TW, NEXP])
        oh = sb("oh", [P, 2, TW, NEXP])
        chosen = sb("chosen", [P, TW, NEXP], BF16)
        mx = sb("mx", [P, 4, TW])
        dm = sb("dm", [P, TW])
        ex = sb("ex", [P, TW])
        incl = sb("incl", [P, NEXP, TW])
        rank = sb("rank", [P, NEXP, TW])
        cmp = sb("cmp", [P, NEXP, TW])
        nblk = sb("nblk", [P, NEXP])
        bend = sb("bend", [P, NEXP])
        bstart = sb("bstart", [P, NEXP])
        bcmp = sb("bcmp", [1, NB, NEXP])
        bsum = sb("bsum", [1, NB])
        pos = sb("pos", [P, 2, TW])
        idx = sb("idx", [P, 2, 2, TW], I32)
        gate = sb("gate", [P, 2, 2, TW])
        block_expert = sb("block_expert", [1, 2, NB], I32)

        xb = sb("xb", [P, RING, D])
        w1b = sb("w1b", [P, RING, FF + 2])
        xbT = sb("xbT", [P, 2, P])
        hb = sb("hb", [P, 2, 2, P])
        yb = sb("yb", [P, RING, D])
        yg = sb("yg", [P, 2, TW, D])

        un = sb("un", [P, TW, D])
        unT = sb("unT", [P, TW * P])
        r1 = sb("r1", [P, TW])
        dtx = sb("dtx", [P, CH, BW, NHEADS])
        dta = sb("dta", [P, CH, BW, NHEADS])
        dte = sb("dte", [P, CH, BW, NHEADS])
        dtu = sb("dtu", [P, CH, BW, NHEADS])
        dtl = sb("dtl", [P, CH, BW, NHEADS])
        dtr = sb("dtr", [P, CH, BW, NHEADS])
        dt_t = sb("dt_t", [P, CH, BW, NHEADS])
        a_t = sb("a_t", [P, CH, BW, NHEADS])
        cs_t = sb("cs_t", [P, CH * BW * NHEADS])
        ncs_t = sb("ncs_t", [P, CH, BW, NHEADS])
        cs_r = sb("cs_r", [CH * BW * NHEADS, P])
        csb = sb("csb", [P, CH, BW * NHEADS, P])
        acc = sb("acc", [P, 2, 2 * SEQ])
        xbc = sb("xbc", [P, 4, BW * SEQ])
        zs = sb("zs", [P, 2, BW * SEQ])
        xdt = sb("xdt", [P, 2, CH, NHEADS, HEADDIM])
        gm = sb("gm", [P, 2, 3, P])
        decay = sb("decay", [P, 2, 3 * NHEADS * P])
        mix = sb("mix", [P, 2, 3 * NHEADS * P])
        yz = sb("yz", [P, 2, 2, SEQ])
        sq = sb("sq", [P, 2, 2, SEQ])
        ss = sb("ss", [P, 2, SEQ])
        o_sb = sb("o_sb", [P, BW, 2 * D + 2 * 64])

        bank = [ctx.enter_context(nc.psum_tensor(f"bank{i}", [P, 512], F32)) for i in range(8)]

        def per_pass(name):
            return [sem(f"{name}_pass{p}") for p in range(2)]

        def per_pair(name):
            return [[sem(f"{name}_pass{p}_pair{s}") for s in range(PAIRS)] for p in range(2)]

        weights_loaded = sem("weights_loaded")
        pool_consts = sem("pool_consts")
        pool_fill = sem("pool_fill")
        sorted_zeroed = sem("sorted_zeroed")
        fixed_dve = sem("fixed_dve")
        fixed_act = sem("fixed_act")
        sp_past = sem("sp_past")
        pool_past = sem("pool_past")
        dve_past = sem("dve_past")
        x_loaded = sem("x_loaded")
        d_chain = per_pass("d_chain")
        d_xn = per_pass("d_xn")
        d_T = per_pass("d_T")
        d_xT = per_pass("d_xT")
        d_logits = per_pass("d_logits")
        d_margin = per_pass("d_margin")
        d_exp = per_pass("d_exp")
        d_chosen = per_pass("d_chosen")
        d_rank = per_pass("d_rank")
        d_plan = per_pass("d_plan")
        scattered = per_pass("scattered")
        w1_loaded = per_pair("w1_loaded")
        xb_loaded = per_pair("xb_loaded")
        y_stored = per_pair("y_stored")
        e_T = per_pass("e_T")
        e_xT = per_pass("e_xT")
        e_H = per_pass("e_H")
        e_h = per_pass("e_h")
        e_Y = per_pass("e_Y")
        e_y = per_pass("e_y")
        gathered = per_pass("gathered")
        c_chain = per_pass("c_chain")
        c_x = per_pass("c_x")
        out_stored = sem("out_stored")
        m_chain = sem("m_chain")
        m_u = sem("m_u")
        m_T = sem("m_T")
        m_uT = sem("m_uT")
        m_dt = sem("m_dt")
        m_abs = sem("m_abs")
        m_exp = sem("m_exp")
        m_one = sem("m_one")
        m_log = sem("m_log")
        m_a = sem("m_a")
        m_cs = sem("m_cs")
        m_cst = sem("m_cst")
        m_csT = sem("m_csT")
        m_csr = sem("m_csr")
        cs_stored = sem("cs_stored")
        cs_loaded = sem("cs_loaded")
        p_xbc = sem("p_xbc")
        p_z = sem("p_z")
        p_acc = sem("p_acc")
        p_older = sem("p_older")
        p_tap = sem("p_tap")
        p_silu = sem("p_silu")
        p_zs = sem("p_zs")
        b_chain = sem("b_chain")
        b_T = sem("b_T")
        b_G = sem("b_G")
        b_xdt = sem("b_xdt")
        b_gm = sem("b_gm")
        b_decay = sem("b_decay")
        b_mix = sem("b_mix")
        b_Y = sem("b_Y")
        b_yz = sem("b_yz")
        b_sq = sem("b_sq")
        b_ss = sem("b_ss")
        b_O = sem("b_O")
        b_o = sem("b_o")
        b_x = sem("b_x")

        WEIGHT_DMAS = 17
        POOL_CONSTS = 10

        def consts_ready(eng):
            eng.wait_ge(weights_loaded, 16 * WEIGHT_DMAS)
            eng.wait_ge(pool_consts, POOL_CONSTS)
            eng.wait_ge(fixed_dve, 3)
            eng.wait_ge(fixed_act, 1)

        def step_past(eng, marker):
            eng.sem_inc(marker, 1)

        def decay_view(s):
            first = s[:, 0:NHEADS * SEQ].rearrange("p (h l) -> p h l", h=NHEADS)
            second = s[:, NHEADS * SEQ:].rearrange("p (h l) -> p h l", h=NHEADS)
            return first, second

        FIRST, LOOP_FROM, LOOP_TO, LAST = -2, 2, NW - 2, NW + 1

        def has(v):
            return not isinstance(v, int) or 0 <= v < NW

        def count(v):
            return min(max(v, 0), NW) if isinstance(v, int) else v

        def wait_past(eng, semaphore, value):
            if not isinstance(value, int) or value > 0:
                eng.wait_ge(semaphore, value)

        def run_steps(eng, step):
            for k in range(FIRST, LOOP_FROM):
                step(k)
            with eng.Fori(LOOP_FROM, LOOP_TO) as k:
                step(k)
            for k in range(LOOP_TO, LAST + 1):
                step(k)

        block = ctx.enter_context(nc.Block())

        @block.sync
        def _(sp):
            def load_x(v):
                sp.dma_start(X[:, bass.ds(v * TW, TW), :], x_rows[:, bass.ds(v * TW, TW), :]).then_inc(x_loaded, 16)

            load_x(0)
            sp.wait_ge(pool_fill, 1)
            loads = [
                (wr_pad[:, 0:NEXP], wr), (br_sb[:], br.partition_broadcast(P)),
                (lng_sb[:], ln_g), (lnb_sb[:], ln_b),
                (dtb_sb[:], dt_bias.partition_broadcast(P)), (aneg_sb[:], a_log.partition_broadcast(P)),
                (conv_w_sb[:], conv_w), (conv_b_sb[:], conv_b), (normw_sb[:], norm_w),
                (w1_sb[:, :, 0:FF], w1.rearrange("e h f -> h e f")), (w1_sb[:, :, FF:FF + 2], b1),
                (w2_sb[:], w2.rearrange("e (m p) n -> p (e m) n", p=P)),
                (b2_sb[:], b2.partition_broadcast(P)),
                (w_in_sb[:], w_in_t), (w_out_sb[:], w_out_t.rearrange("(m p) n -> p m n", p=P)),
            ]
            for dst, src in loads:
                sp.dma_start(dst, src).then_inc(weights_loaded, 16)
            for g in range(2):
                sp.dma_start(dskip_sb[64 * g:64 * g + 64, :], dskip[g].partition_broadcast(64)).then_inc(weights_loaded, 16)
            sp.wait_ge(pool_fill, 2)
            zero = yg[:].rearrange("p k i d -> p (k i) d")
            for p in range(2):
                rows = sorted_in[p].rearrange("(k p) d -> p k d", p=P)
                for a in range(0, NB, 2 * TW):
                    k = min(2 * TW, NB - a)
                    sp.dma_start(rows[:, a:a + k, :], zero[:, 0:k, :]).then_inc(sorted_zeroed, 16)
            load_x(1)
            load_x(2)

            def wait_sp(semaphore, value):
                wait_past(sp, semaphore, value)
                step_past(sp, sp_past)

            def load(v, p, q, s):
                sp.dma_start(xb[:, 2 * s:2 * s + 2, :],
                             sorted_in[p][bass.ds(q * 2 * P, 2 * P), :].rearrange("(a p) d -> p a d", p=P)
                             ).then_inc(xb_loaded[p][s], 16)
                for a in range(2):
                    e = sp.value_load(block_expert[0:1, p, bass.ds(2 * q + a, 1)], min_val=0, max_val=NEXP - 1)
                    sp.dma_start(w1b[:, 2 * s + a, :], w1_sb[:, bass.ds(e, 1), :]).then_inc(w1_loaded[p][s], 16)

            def store(v, p, q, s):
                wait_sp(e_y[p], v * NB + 2 * q + 2)
                sp.dma_start(sorted_out[p][bass.ds(q * 2 * P, 2 * P), :].rearrange("(a p) d -> p a d", p=P),
                             yb[:, 2 * s:2 * s + 2, :]).then_inc(y_stored[p][s], 16)

            def sources_ready(v, p):
                wait_sp(d_plan[p], v + 1)
                wait_sp(scattered[p], 256 * (v + 1))

            def first_loads(v, p):
                sources_ready(v, p)
                for s in range(PAIRS):
                    load(v, p, s, s)

            def experts(v, p, next_v):
                wait_sp(gathered[p], 256 * v)
                with sp.Fori(0, ROUNDS - 1) as r:
                    for s in range(PAIRS):
                        wait_sp(e_h[p], v * NB + r * RING + 2 * s + 2)
                        load(v, p, r * PAIRS + s + PAIRS, s)
                        store(v, p, r * PAIRS + s, s)
                if next_v is not None:
                    sources_ready(next_v, 1 - p)
                for s in range(PAIRS):
                    q = NB // 2 - PAIRS + s
                    if next_v is not None:
                        wait_sp(e_h[p], v * NB + 2 * q + 2)
                        load(next_v, 1 - p, s, s)
                    store(v, p, q, s)

            def step(k):
                if has(k + 1):
                    if not has(k - 2):
                        first_loads(k + 1, 0)
                    experts(k + 1, 0, None)
                if has(k - 2):
                    wait_sp(c_x[1], TW * (k - 1))
                    sp.dma_start(out_rows[:, bass.ds((k - 2) * TW, TW), :],
                                 X[:, bass.ds((k - 2) * TW, TW), :]).then_inc(out_stored, 16)
                if has(k + 3) and not (isinstance(k, int) and k < 0):
                    load_x(k + 3)
                if has(k - 1):
                    first_loads(k - 1, 1)
                    experts(k - 1, 1, k + 2 if has(k + 2) else None)

            for k in range(FIRST, LOOP_FROM):
                step(k)
            with sp.Fori(LOOP_FROM, LOOP_TO - 1) as k:
                step(k)
            for k in range(LOOP_TO - 1, LAST + 1):
                step(k)
            sp.wait_ge(out_stored, 16 * NW)

        @block.gpsimd
        def _(pool):
            pool.memset(wr_pad[:], 0.0).then_inc(pool_fill, 1)
            pool.memset(yg[:], 0.0).then_inc(pool_fill, 1)
            pool.memset(ident[:], 0.0).then_inc(pool_consts, 1)
            pool.memset(ones[:], 1.0).then_inc(pool_consts, 1)
            pool.memset(ones_bf[:], 1.0).then_inc(pool_consts, 1)
            pool.memset(causal[:, 1, :], 1.0).then_inc(pool_consts, 1)
            pool.wait_ge(pool_consts, 4)
            pool.affine_select(out=ident[:], in_=ident[:], compare_op=ALU.not_equal, fill=1.0, base=0,
                               pattern=[[-1, P]], channel_multiplier=1).then_inc(pool_consts, 1)
            for dst in (upper[:], causal[:, 0, :], causal[:, 2, :]):
                pool.affine_select(out=dst, in_=ones[:], compare_op=ALU.is_ge, fill=0.0, base=0,
                                   pattern=[[1, P]], channel_multiplier=-1).then_inc(pool_consts, 1)
            pool.affine_select(out=below_bf[:], in_=ones_bf[:], compare_op=ALU.is_ge, fill=0.0, base=-1,
                               pattern=[[1, P]], channel_multiplier=-1).then_inc(pool_consts, 1)

            def numbers(dst, parts, base, pattern, n):
                if n:
                    pool.wait_ge(pool_fill, 2 + 2 * n)
                pool.iota(itmp[0:parts, 0:dst.free_size()], pattern=pattern, base=base,
                          channel_multiplier=0).then_inc(pool_fill, 1)
                pool.wait_ge(pool_fill, 3 + 2 * n)
                pool.tensor_copy(dst, itmp[0:parts, 0:dst.free_size()]).then_inc(pool_fill, 1)

            numbers(expert_rev[:].rearrange("p i e -> p (i e)"), P, NEXP, [[0, TW], [-1, NEXP]], 0)
            numbers(tile_start[:].rearrange("p e j -> p (e j)"), P, 0, [[0, NEXP], [P, TW]], 1)
            numbers(block_no[:].rearrange("p k e -> p (k e)"), 1, 0, [[1, NB], [0, NEXP]], 2)
            pool.memset(not_first[:], 1.0).then_inc(pool_fill, 1)
            pool.wait_ge(pool_fill, 9)
            pool.memset(not_first[:, :, 0:1], 0.0).then_inc(pool_consts, 1)
            pool.wait_ge(sorted_zeroed, 16 * 2 * -(-NB // (2 * TW)))

            def scatter(v, p):
                pool.wait_ge(d_plan[p], v + 1)
                wait_past(pool, e_T[p], v * NB)
                step_past(pool, pool_past)
                for k in range(2):
                    for i in range(TW):
                        pool.indirect_dma_start(
                            out=sorted_in[p], out_offset=bass.IndirectOffsetOnAxis(ap=idx[:, p, k, i:i + 1], axis=0),
                            in_=xn[:, p, i, :], in_offset=None).then_inc(scattered[p], 16)

            def gather(v, p, other):
                for s in range(PAIRS):
                    pool.wait_ge(y_stored[p][s], 16 * ROUNDS * (v + 1))
                wait_past(pool, c_x[p], TW * v)
                wait_past(pool, c_x[1 - p], TW * count(other))
                step_past(pool, pool_past)
                for k in range(2):
                    for i in range(TW):
                        pool.indirect_dma_start(
                            out=yg[:, k, i, :], out_offset=None, in_=sorted_out[p],
                            in_offset=bass.IndirectOffsetOnAxis(ap=idx[:, p, k, i:i + 1], axis=0)).then_inc(gathered[p], 16)

            def step(k):
                if has(k - 2):
                    gather(k - 2, 1, k + 1)
                if has(k + 1):
                    gather(k + 1, 0, k - 1)
                if has(k - 1):
                    scatter(k - 1, 1)
                if has(k + 2):
                    scatter(k + 2, 0)

            run_steps(pool, step)

        @block.scalar
        def _(act):
            act.wait_ge(weights_loaded, 16 * WEIGHT_DMAS)
            act.activation(aneg_sb[:], aneg_sb[:], ACT.Exp).then_inc(fixed_act, 1)
            consts_ready(act)

            def route(v, p):
                for half in range(2):
                    act.wait_ge(d_T[p], 2 * v + half + 1)
                    act.activation(xnT[:, 512 * half:512 * half + 512], bank[6][:], ACT.Copy).then_inc(d_xT[p], 1)
                    yield
                act.wait_ge(d_margin[p], v + 1)
                act.activation(ex[:], dm[:], ACT.Exp).then_inc(d_exp[p], 1)

            def prepare(v):
                for half in range(2):
                    act.wait_ge(m_T, 2 * v + half + 1)
                    act.activation(unT[:, 512 * half:512 * half + 512], bank[6][:], ACT.Identity,
                                   bias=lnb_sb[:], scale=lng_sb[:]).then_inc(m_uT, 1)
                    yield
                act.wait_ge(m_abs, v + 1)
                act.activation(dte[:], dta[:], ACT.Exp, scale=-1.0).then_inc(m_exp, 1)
                yield
                act.wait_ge(m_one, v + 1)
                act.activation(dtl[:], dtu[:], ACT.Ln).then_inc(m_log, 1)
                yield
                act.wait_ge(m_csT, v + 1)
                wait_past(act, cs_loaded, 16 * v)
                act.activation(cs_r[:], bank[7][0:CH * BW * NHEADS, 0:P], ACT.Copy).then_inc(m_csr, 1)
                act.wait_ge(m_csr, v + 1)
                act.dma_start(cs_dram, cs_r[:]).then_inc(cs_stored, 16)
                yield
                act.wait_ge(cs_stored, 16 * (v + 1))
                act.dma_start(csb[:].rearrange("p c k l -> p (c k l)"),
                              cs_dram.rearrange("r l -> (r l)").partition_broadcast(P)).then_inc(cs_loaded, 16)

            def experts(v, p, done, side, at):
                for q in range(2):
                    wait_past(act, e_Y[q], NB * done[q])

                def take_x(b):
                    act.wait_ge(e_T[p], v * NB + b + 1)
                    if b >= 2:
                        act.wait_ge(e_H[p], v * NB + b - 1)
                    act.activation(xbT[:, b % 2, :], bank[b % 2][:, 0:P], ACT.Copy).then_inc(e_xT[p], 1)

                def hidden(b):
                    act.wait_ge(e_H[p], v * NB + b + 1)
                    if b >= 2:
                        act.wait_ge(e_Y[p], v * NB + b - 1)
                    for f in range(2):
                        ins = act.activation(hb[:, b % 2, f, :], bank[2 + b % 2][:, P * f:P * f + P], ACT.Relu,
                                             bias=w1b[:, b % RING, FF + f:FF + f + 1])
                    ins.then_inc(e_h[p], 1)

                take_x(0)
                for b in range(NB):
                    if b + 1 < NB:
                        take_x(b + 1)
                    hidden(b)
                    advance(side, at.count(b))
                finish(side)

            def project(w):
                def silu(k):
                    act.wait_ge(p_tap, 8 * w + k + 1)
                    act.activation(xbc[:, k % 4, 512 * (k // 4):512 * (k // 4) + 512], acc[:, k % 2, :],
                                   ACT.Silu).then_inc(p_silu, 1)

                for q in range(2):
                    for i in range(4):
                        k = 4 * q + i
                        act.wait_ge(p_xbc, 8 * w + k + 1)
                        if k >= 2:
                            act.wait_ge(p_silu, 8 * w + k - 1)
                        act.activation(acc[:, k % 2, :], bank[k % 4][:], ACT.Identity, bias=conv_b_sb[:, i:i + 1],
                                       scale=conv_w_sb[:, i, D_CONV - 1:D_CONV]).then_inc(p_acc, 1)
                        if k >= 1:
                            silu(k - 1)
                    if q == 1:
                        silu(7)
                    for m in range(2):
                        act.wait_ge(p_z, 4 * w + 2 * q + m + 1)
                        act.activation(zs[:, m, 512 * q:512 * q + 512], bank[4 + m][:], ACT.Silu).then_inc(p_zs, 1)

            def mixer(w, side):
                def decays(j):
                    if j == 0:
                        act.wait_ge(cs_loaded, 16 * (w + 1))
                    wait_past(act, b_mix, 2 * (BW * w + j - 1))
                    first, second = decay_view(decay[:, j % 2, :])
                    for h in range(NHEADS):
                        act.activation(first[:, h, :].rearrange("p (c l) -> p c l", c=CH),
                                       csb[:, :, j * NHEADS + h, :], ACT.Exp,
                                       bias=ncs_t[:, 0, j, h:h + 1]).then_inc(b_decay, 1)
                    for h in range(NHEADS):
                        act.activation(second[:, h, :], csb[:, 1, j * NHEADS + h, :], ACT.Exp,
                                       bias=ncs_t[:, 1, j, h:h + 1]).then_inc(b_decay, 1)

                def square(j):
                    act.wait_ge(b_yz, BW * w + j + 1)
                    wait_past(act, b_ss, BW * w + j - 1)
                    act.activation(sq[:, j % 2], yz[:, j % 2], ACT.Square).then_inc(b_sq, 1)

                def take_out(j):
                    act.wait_ge(b_O, BW * w + j + 1)
                    act.activation(o_sb[:, j, :], bank[4 + j % 2][:, 0:2 * D + 2 * 64], ACT.Copy).then_inc(b_o, 1)

                project(w)
                advance(side)
                decays(0)
                advance(side)
                wait_past(act, b_x, TW * w)
                for j in range(BW):
                    if j + 1 < BW:
                        decays(j + 1)
                    square(j)
                    if j >= 1:
                        take_out(j - 1)
                    if j == 1:
                        advance(side)
                take_out(BW - 1)
                finish(side)

            def step(k):
                side = route(k - 1, 1) if has(k - 1) else iter(())
                if has(k + 1):
                    experts(k + 1, 0, (count(k + 1), count(k - 1)), side, ROUTE_AT)
                finish(side)
                side = route(k + 2, 0) if has(k + 2) else iter(())
                if has(k):
                    mixer(k, side)
                finish(side)
                side = prepare(k + 1) if has(k + 1) else iter(())
                if has(k - 1):
                    experts(k - 1, 1, (count(k + 2), count(k - 1)), side, PREPARE_AT)
                finish(side)

            ROUTE_AT = (10, 12, 17)
            PREPARE_AT = (14, 16, 17, 18, 22)
            run_steps(act, step)

        @block.tensor
        def _(pe):
            consts_ready(pe)

            def small_banks_free(plans0, plans1, prepared):
                wait_past(pe, d_plan[0], count(plans0))
                wait_past(pe, d_plan[1], count(plans1))
                wait_past(pe, m_chain, count(prepared) * MIX0_STEPS)
                wait_past(pe, m_csr, count(prepared))

            def route(v, p, used):
                small_banks_free(*used)
                for half in range(2):
                    if half == 1:
                        pe.wait_ge(d_xT[p], 2 * v + 1)
                    pe.wait_ge(d_xn[p], TW * v + 4 * half + 4)
                    for i in range(4):
                        mm = pe.transpose(bank[6][:, P * i:P * i + P], xn[:, p, 4 * half + i, :], ident[:])
                    mm.then_inc(d_T[p], 1)
                    yield
                for half in range(2):
                    pe.wait_ge(d_xT[p], 2 * v + half + 1)
                    for i in range(4 * half, 4 * half + 4):
                        mm = pe.matmul(bank[7][:, 64 * i:64 * i + 64], xnT[:, P * i:P * i + P], wr_pad[:],
                                       start=True, stop=True)
                mm.then_inc(d_logits[p], 1)
                yield
                pe.wait_ge(d_chosen[p], v + 1)
                by_expert = chosen[:].rearrange("p i e -> p e i")
                pe.matmul(bank[6][:, 0:64], below_bf[:], by_expert, start=True, stop=True)
                pe.matmul(bank[6][:, 64:128], ones_bf[:], by_expert, start=True, stop=True).then_inc(d_rank[p], 1)

            def prepare(v, used):
                small_banks_free(*used)
                for half in range(2):
                    pe.wait_ge(m_u, TW * v + 4 * half + 4)
                    if half == 1:
                        pe.wait_ge(m_uT, 2 * v + 1)
                    for i in range(4):
                        mm = pe.transpose(bank[6][:, P * i:P * i + P], un[:, 4 * half + i, :], ident[:])
                    mm.then_inc(m_T, 1)
                    yield
                pe.wait_ge(m_uT, 2 * v + 2)
                for i in range(TW):
                    mm = pe.matmul(bank[7][:, 64 * i:64 * i + 64], unT[:, P * i:P * i + P],
                                   w_in_sb[:, NPROJ - 64:NPROJ], start=True, stop=True)
                mm.then_inc(m_dt, 1)
                yield
                pe.wait_ge(m_a, v + 1)
                half = BW * NHEADS
                a_rows = a_t[:].rearrange("p c j h -> p (c j h)")
                pe.matmul(bank[6][:, 0:2 * half], upper[:], a_rows, start=True, stop=False)
                pe.matmul(bank[6][:, half:2 * half], ones[:], a_rows[:, 0:half], start=False,
                          stop=True).then_inc(m_cs, 1)
                yield
                pe.wait_ge(m_cst, v + 1)
                pe.transpose(bank[7][0:2 * half, 0:P], cs_t[:], ident[:]).then_inc(m_csT, 1)

            def banks_free(done):
                for q in range(2):
                    wait_past(pe, e_y[q], NB * done[q])
                wait_past(pe, b_o, BW * done[2])

            def experts(v, p, done, side, at):
                banks_free(done)
                pe.wait_ge(d_plan[p], v + 1)

                def turn_x(b):
                    if b % 2 == 0:
                        pe.wait_ge(xb_loaded[p][b % RING // 2], 16 * (ROUNDS * v + b // RING + 1))
                    if b >= 2:
                        pe.wait_ge(e_xT[p], v * NB + b - 1)
                    pe.transpose(bank[b % 2][:, 0:P], xb[:, b % RING, :], ident[:]).then_inc(e_T[p], 1)

                def up(b):
                    if b % 2 == 0:
                        pe.wait_ge(w1_loaded[p][b % RING // 2], 32 * (ROUNDS * v + b // RING + 1))
                    pe.wait_ge(e_xT[p], v * NB + b + 1)
                    if b >= 2:
                        pe.wait_ge(e_h[p], v * NB + b - 1)
                    for f in range(2):
                        mm = pe.matmul(bank[2 + b % 2][:, P * f:P * f + P], w1b[:, b % RING, P * f:P * f + P],
                                       xbT[:, b % 2, :], start=True, stop=True)
                    mm.then_inc(e_H[p], 1)

                def down(b):
                    e = pe.value_load(block_expert[0:1, p, b:b + 1], min_val=0, max_val=NEXP - 1)
                    pe.wait_ge(e_h[p], v * NB + b + 1)
                    if b >= 2:
                        pe.wait_ge(e_y[p], v * NB + b - 1)
                    for f in range(2):
                        mm = pe.matmul(bank[4 + b % 2][:, 0:P], hb[:, b % 2, f, :],
                                       w2_sb[:, bass.ds(2 * e + f, 1), :].rearrange("p a d -> p (a d)"),
                                       start=(f == 0), stop=(f == 1))
                    mm.then_inc(e_Y[p], 1)

                turn_x(0)
                turn_x(1)
                up(0)
                for b in range(NB):
                    if b + 2 < NB:
                        turn_x(b + 2)
                    if b + 1 < NB:
                        up(b + 1)
                    down(b)
                    advance(side, at.count(b))
                finish(side)

            def mixer(w, done, side):
                banks_free(done)
                for q in range(2):
                    for i in range(4):
                        k = 4 * q + i
                        if k >= 4:
                            pe.wait_ge(p_tap, 8 * w + k - 3)
                        pe.matmul(bank[k % 4][:], w_in_sb[:, XCOL + P * i:XCOL + P * i + P],
                                  unT[:, 512 * q:512 * q + 512], start=True, stop=True).then_inc(p_xbc, 1)
                    for m in range(2):
                        if q == 1:
                            pe.wait_ge(p_zs, 4 * w + m + 1)
                        pe.matmul(bank[4 + m][:], w_in_sb[:, ZCOL + P * m:ZCOL + P * m + P],
                                  unT[:, 512 * q:512 * q + 512], start=True, stop=True).then_inc(p_z, 1)

                def sources(j):
                    wait_past(pe, b_xdt, BW * w + j)
                    for c in range(CH):
                        for m in range(2):
                            t = SEQ * j + P * c
                            mm = pe.transpose(bank[0][:, 256 * c + P * m:256 * c + P * m + P],
                                              xbc[:, m, t:t + P], ident[:])
                    mm.then_inc(b_T, 1)
                    wait_past(pe, b_gm, BW * w + j)
                    t = SEQ * j
                    pe.matmul(bank[1][:, 0:SEQ], xbc[:, 2, t:t + P], xbc[:, 3, t:t + SEQ], start=True, stop=True)
                    pe.matmul(bank[1][:, SEQ:SEQ + P], xbc[:, 2, t + P:t + SEQ], xbc[:, 3, t + P:t + SEQ],
                              start=True, stop=True).then_inc(b_G, 1)

                def outputs(j):
                    pe.wait_ge(b_mix, 2 * (BW * w + j + 1))
                    wait_past(pe, b_yz, BW * w + j - 1)
                    first, second = decay_view(mix[:, j % 2, :])
                    for h in range(NHEADS):
                        a = HEADDIM * (h % 2)
                        o = bank[2 + j % 2][a:a + HEADDIM, SEQ * (h // 2):SEQ * (h // 2) + SEQ]
                        pe.matmul(o, xdt[:, j % 2, 0, h, :], first[:, h, :], start=True, stop=False)
                        mm = pe.matmul(o[:, P:SEQ], xdt[:, j % 2, 1, h, :], second[:, h, :], start=False, stop=True)
                    mm.then_inc(b_Y, 1)

                def project_out(j):
                    pe.wait_ge(b_ss, BW * w + j + 1)
                    wait_past(pe, b_o, BW * w + j - 1)
                    o = bank[4 + j % 2]
                    for c in range(CH):
                        for m in range(2):
                            pe.matmul(o[:, D * c:D * c + D], yz[:, j % 2, m, P * c:P * c + P], w_out_sb[:, m, :],
                                      start=(m == 0), stop=(m == 1))
                        mm = pe.matmul(o[:, 2 * D + 64 * c:2 * D + 64 * c + 64], ss[:, j % 2, P * c:P * c + P],
                                       ones[:, 0:64], start=True, stop=True)
                    mm.then_inc(b_O, 1)

                advance(side)
                pe.wait_ge(p_silu, 8 * (w + 1))
                pe.wait_ge(p_tap, 8 * (w + 1))
                sources(0)
                advance(side)
                sources(1)
                advance(side)
                outputs(0)
                for j in range(BW):
                    if j + 2 < BW:
                        sources(j + 2)
                    if j + 1 < BW:
                        outputs(j + 1)
                    project_out(j)
                    if j == 1:
                        advance(side)
                finish(side)

            def step(k):
                side = route(k - 1, 1, (k + 2, k - 1, k + 1)) if has(k - 1) else iter(())
                if has(k + 1):
                    experts(k + 1, 0, (count(k + 1), count(k - 1), count(k)), side, ROUTE_AT)
                finish(side)
                side = route(k + 2, 0, (k + 2, k, k + 1)) if has(k + 2) else iter(())
                if has(k):
                    mixer(k, (count(k + 2), count(k - 1), count(k)), side)
                finish(side)
                side = prepare(k + 1, (k + 3, k, k + 1)) if has(k + 1) else iter(())
                if has(k - 1):
                    experts(k - 1, 1, (count(k + 2), count(k - 1), count(k + 1)), side, PREPARE_AT)
                finish(side)

            ROUTE_AT = (10, 12, 13, 17)
            PREPARE_AT = (14, 16, 17, 20, 22)
            run_steps(pe, step)

        @block.vector
        def _(dve):
            dve.wait_ge(weights_loaded, 16 * WEIGHT_DMAS)
            dve.wait_ge(fixed_act, 1)
            dve.tensor_scalar(aneg_sb[:], aneg_sb[:], -1.0, None, ALU.mult).then_inc(fixed_dve, 1)
            for m in range(2):
                dve.tensor_scalar(w_out_sb[:, m, :], w_out_sb[:, m, :], normw_sb[:, m:m + 1], None,
                                  ALU.mult).then_inc(fixed_dve, 1)
            consts_ready(dve)

            def rsqrt(ch, bufs):
                v, i, h, t, yi = (b[:] for b in bufs)
                y = yi.bitcast(F32)
                yield from ch.link(dve.tensor_scalar(i, v.bitcast(I32), 1, None, ALU.logical_shift_right))
                yield from ch.link(dve.tensor_scalar(yi, i, -1.0, float(MAGIC), ALU.mult, ALU.add))
                yield from ch.link(dve.tensor_scalar(h, v, -0.5, None, ALU.mult))
                for _ in range(3):
                    yield from ch.link(dve.tensor_tensor(t, y, y, ALU.mult))
                    yield from ch.link(dve.tensor_tensor(t, t, h, ALU.mult))
                    yield from ch.link(dve.scalar_tensor_tensor(y, t, 1.5, y, ALU.add, ALU.mult))

            rs = (rs_v, rs_i, rs_h, rs_t, rs_y)
            fin = (fin_v, fin_i, fin_h, fin_t, fin_y)

            def x_tile(w, i):
                return X[:, bass.ds(w * TW + i, 1), :].rearrange("p a d -> p (a d)")

            def moments(ch, v):
                for i in range(TW):
                    ch.mark(dve.bn_stats(stats[:, i, :], x_tile(v, i)))
                    yield
                ch.settle()
                step_past(dve, dve_past)
                for i in range(TW):
                    ch.mark(dve.bn_aggr(mv[:, i, :], stats[:, i, :]))
                    yield
                ch.settle()
                yield from ch.link(dve.tensor_scalar(rs_v[:], mv[:, :, 1], EPS, None, ALU.add))

            def over_experts(a):
                return a.unsqueeze(2).broadcast_to([P, TW, NEXP])

            def route(v, p, between):
                if p == 0:
                    dve.wait_ge(x_loaded, 16 * (v + 1))
                    step_past(dve, dve_past)
                ch = Chain(dve, d_chain[p], v * DISPATCH_STEPS)
                yield from moments(ch, v)
                yield from rsqrt(ch, rs)
                y = rs_y[:].bitcast(F32)
                wait_past(dve, scattered[p], 256 * v)
                for i in range(TW):
                    dve.tensor_scalar(xn[:, p, i, :], x_tile(v, i), mv[:, i, 0:1], y[:, i:i + 1],
                                      ALU.subtract, ALU.mult).then_inc(d_xn[p], 1)
                    yield
                yield from between
                dve.wait_ge(d_logits[p], v + 1)
                logits = bank[7][:].rearrange("p (i e) -> p i e", i=TW)[:, :, 0:NEXP]
                yield from ch.link(dve.tensor_tensor(lg[:], logits, br_sb[:].unsqueeze(1).broadcast_to([P, TW, NEXP]),
                                                     ALU.add))
                src = lg
                for k in range(2):
                    yield from ch.link(dve.tensor_reduce(mx[:, 2 * k, :], src[:], AX.X, ALU.max))
                    yield from ch.link(dve.tensor_tensor(sc[:], src[:], over_experts(mx[:, 2 * k, :]), ALU.is_equal))
                    yield from ch.link(dve.tensor_tensor(sc[:], sc[:], expert_rev[:], ALU.mult))
                    yield from ch.link(dve.tensor_reduce(mx[:, 2 * k + 1, :], sc[:], AX.X, ALU.max))
                    yield from ch.link(dve.tensor_tensor(oh[:, k], expert_rev[:], over_experts(mx[:, 2 * k + 1, :]),
                                                         ALU.is_equal))
                    if k == 0:
                        yield from ch.link(dve.scalar_tensor_tensor(lg2[:], oh[:, 0], -HUGE, lg[:], ALU.mult, ALU.add))
                        src = lg2
                dve.tensor_tensor(chosen[:], oh[:, 0], oh[:, 1], ALU.add).then_inc(d_chosen[p], 1)
                dve.tensor_tensor(dm[:], mx[:, 2, :], mx[:, 0, :], ALU.subtract).then_inc(d_margin[p], 1)
                yield
                dve.wait_ge(d_exp[p], v + 1)
                yield from ch.link(dve.tensor_scalar(rs_t[:], ex[:], 2.0, 2.0, ALU.mult, ALU.add))
                yield from ch.link(dve.reciprocal(gate[:, p, 0, :], rs_t[:]))
                ch.mark(dve.tensor_tensor(gate[:, p, 1, :], gate[:, p, 0, :], ex[:], ALU.mult))
                yield
                dve.wait_ge(d_rank[p], v + 1)
                before = bank[6][:, 0:64].rearrange("p (e i) -> p e i", e=NEXP)
                total = bank[6][:, 64:128].rearrange("p (e i) -> p e i", e=NEXP)
                yield from ch.link(dve.tensor_tensor_scan(incl[:].rearrange("p e i -> p (e i)"),
                                                          not_first[:].rearrange("p e i -> p (e i)"),
                                                          bank[6][:, 64:128], 0.0, ALU.mult, ALU.add))
                yield from ch.link(dve.tensor_tensor(rank[:], incl[:], total, ALU.subtract))
                yield from ch.link(dve.tensor_tensor(rank[:], rank[:], before, ALU.add))
                yield from ch.link(dve.tensor_tensor(cmp[:], incl[:, :, TW - 1:TW].broadcast_to([P, NEXP, TW]),
                                                     tile_start[:], ALU.is_gt))
                yield from ch.link(dve.tensor_reduce(nblk[:], cmp[:], AX.X, ALU.add))
                yield from ch.link(dve.tensor_tensor_scan(bend[:], ones[:, 0:NEXP], nblk[:], 0.0, ALU.mult, ALU.add))
                yield from ch.link(dve.tensor_tensor(bstart[:], bend[:], nblk[:], ALU.subtract))
                yield from ch.link(dve.scalar_tensor_tensor(rank[:], bstart[:].unsqueeze(2).broadcast_to([P, NEXP, TW]),
                                                            float(P), rank[:], ALU.mult, ALU.add))
                by_tile = rank[:].rearrange("p e i -> p i e")
                for k in range(2):
                    yield from ch.link(dve.tensor_tensor(sc[:], oh[:, k], by_tile, ALU.mult))
                    yield from ch.link(dve.tensor_reduce(pos[:, k, :], sc[:], AX.X, ALU.add))
                yield from ch.link(dve.tensor_tensor(bcmp[:], bend[0:1, :].unsqueeze(1).broadcast_to([1, NB, NEXP]),
                                                     block_no[:], ALU.is_le))
                yield from ch.link(dve.tensor_reduce(bsum[:], bcmp[:], AX.X, ALU.add))
                wait_past(dve, gathered[p], 256 * v)
                ch.mark(dve.tensor_scalar(block_expert[0:1, p, :], bsum[:], float(NEXP - 1), None, ALU.min))
                assert ch.k == DISPATCH_STEPS, ch.k
                dve.tensor_copy(idx[:, p], pos[:]).then_inc(d_plan[p], 1)
                dve.wait_ge(d_plan[p], v + 1)
                step_past(dve, dve_past)

            def combine(v, p):
                ch = Chain(dve, c_chain[p], v * COMBINE_STEPS)
                dve.wait_ge(gathered[p], 256 * (v + 1))
                for i in range(TW):
                    ch.mark(dve.scalar_tensor_tensor(x_tile(v, i), yg[:, 0, i, :], gate[:, p, 0, i:i + 1],
                                                     x_tile(v, i), ALU.mult, ALU.add))
                    yield
                ch.settle()
                for i in range(TW):
                    dve.scalar_tensor_tensor(x_tile(v, i), yg[:, 1, i, :], gate[:, p, 1, i:i + 1],
                                             x_tile(v, i), ALU.mult, ALU.add).then_inc(c_x[p], 1)
                    yield
                dve.wait_ge(c_x[p], TW * (v + 1))
                step_past(dve, dve_past)
                assert ch.k == COMBINE_STEPS

            def prepare(v):
                ch = Chain(dve, m_chain, v * MIX0_STEPS)
                step_past(dve, dve_past)
                yield from moments(ch, v)
                yield from rsqrt(ch, rs)
                y = rs_y[:].bitcast(F32)
                yield from ch.link(dve.tensor_copy(r1[:], y))
                yield from ch.link(dve.tensor_tensor(rs_t[:], r1[:], r1[:], ALU.mult))
                yield from ch.link(dve.tensor_tensor(rs_v[:], rs_t[:], mv[:, :, 1], ALU.mult))
                yield from ch.link(dve.tensor_scalar(rs_v[:], rs_v[:], EPS, None, ALU.add))
                yield from rsqrt(ch, rs)
                yield from ch.link(dve.tensor_tensor(rs_h[:], r1[:], y, ALU.mult))
                for i in range(TW):
                    dve.tensor_scalar(un[:, i, :], x_tile(v, i), mv[:, i, 0:1], rs_h[:, i:i + 1],
                                      ALU.subtract, ALU.mult).then_inc(m_u, 1)
                    yield
                yield from ch.link(dve.scalar_tensor_tensor(rs_t[:], mv[:, :, 0], -1.0, r1[:], ALU.mult, ALU.mult))
                yield from ch.link(dve.tensor_scalar(rs_v[:], r1[:], 1.0, None, ALU.add))
                dve.wait_ge(m_u, TW * (v + 1))
                for i in range(TW):
                    ch.mark(dve.tensor_scalar(x_tile(v, i), x_tile(v, i), rs_v[:, i:i + 1], rs_t[:, i:i + 1],
                                              ALU.mult, ALU.add))
                    yield
                dve.wait_ge(m_dt, v + 1)
                raw = bank[7][:].rearrange("p (j c f) -> p c j f", j=BW, c=CH)[:, :, :, 64 - NHEADS:64]
                for c in range(CH):
                    ch.mark(dve.tensor_tensor(dtx[:, c], raw[:, c], dtb_sb[:].unsqueeze(1).broadcast_to([P, BW, NHEADS]),
                                              ALU.add))
                yield
                ch.settle()
                dve.scalar_tensor_tensor(dta[:], dtx[:], -1.0, dtx[:], ALU.mult, ALU.max).then_inc(m_abs, 1)
                yield
                dve.wait_ge(m_exp, v + 1)
                dve.tensor_scalar(dtu[:], dte[:], 1.0, None, ALU.add).then_inc(m_one, 1)
                yield
                dve.wait_ge(m_one, v + 1)
                ch.mark(dve.reciprocal(dtr[:], dtu[:]))
                yield from ch.link(dve.tensor_scalar(dta[:], dtu[:], -1.0, None, ALU.add))
                yield from ch.link(dve.scalar_tensor_tensor(dta[:], dta[:], -1.0, dte[:], ALU.mult, ALU.add))
                yield from ch.link(dve.tensor_tensor(dta[:], dta[:], dtr[:], ALU.mult))
                dve.wait_ge(m_log, v + 1)
                yield from ch.link(dve.tensor_tensor(dta[:], dta[:], dtl[:], ALU.add))
                yield from ch.link(dve.scalar_tensor_tensor(dt_t[:], dtx[:], 0.0, dta[:], ALU.max, ALU.add))
                dve.tensor_tensor(a_t[:].rearrange("p c j h -> p (c j) h"), dt_t[:].rearrange("p c j h -> p (c j) h"),
                                  aneg_sb[:].unsqueeze(1).broadcast_to([P, CH * BW, NHEADS]), ALU.mult).then_inc(m_a, 1)
                yield
                dve.wait_ge(m_cs, v + 1)
                wait_past(dve, b_decay, 8 * BW * v)
                sums = bank[6][:, 0:CH * BW * NHEADS]
                dve.tensor_copy(cs_t[:], sums).then_inc(m_cst, 1)
                yield from ch.link(dve.tensor_scalar(ncs_t[:].rearrange("p c j h -> p (c j h)"), sums, -1.0, None,
                                                     ALU.mult))
                step_past(dve, dve_past)
                assert ch.k == MIX0_STEPS, ch.k

            def experts(v, p, done, side):
                def rows(b):
                    e = dve.value_load(block_expert[0:1, p, b:b + 1], min_val=0, max_val=NEXP - 1)
                    dve.wait_ge(e_Y[p], v * NB + b + 1)
                    s = b % RING
                    if b % 2 == 0 and b >= RING:
                        dve.wait_ge(y_stored[p][s // 2], 16 * (ROUNDS * v + b // RING))
                    elif b % 2 == 0:
                        for q in range(2):
                            wait_past(dve, y_stored[q][s // 2], 16 * ROUNDS * done[q])
                    dve.tensor_tensor(yb[:, s, :].unsqueeze(1), bank[4 + b % 2][:, 0:P].unsqueeze(1),
                                      b2_sb[:, bass.ds(e, 1), :], ALU.add).then_inc(e_y[p], 1)

                dve.wait_ge(d_plan[p], v + 1)
                step_past(dve, dve_past)
                for b in range(NB):
                    rows(b)
                    advance(side, 4)
                finish(side)

            def mixer(w, side):
                for q in range(2):
                    for i in range(4):
                        k = 4 * q + i
                        dve.wait_ge(p_acc, 8 * w + k + 1)
                        a = acc[:, k % 2, :].rearrange("p (j t) -> p j t", j=2)
                        v = bank[k % 4][:].rearrange("p (j t) -> p j t", j=2)
                        for back in range(1, D_CONV):
                            if back > 1:
                                dve.wait_ge(p_older, 16 * w + 2 * k + back - 1)
                            ins = dve.scalar_tensor_tensor(
                                a[:, :, back:], v[:, :, :SEQ - back], conv_w_sb[:, i, D_CONV - 1 - back:D_CONV - back],
                                a[:, :, back:], ALU.mult, ALU.add)
                            ins.then_inc(p_older if back < D_CONV - 1 else p_tap, 1)
                            advance(side, 2 if back < D_CONV - 1 else 1)

                def weights(j):
                    dve.wait_ge(b_T, BW * w + j + 1)
                    wait_past(dve, b_Y, BW * w + j - 1)
                    dve.tensor_tensor(xdt[:, j % 2], bank[0][:].rearrange("p (c h d) -> p c h d", c=CH, h=NHEADS),
                                      dt_t[:, :, j, :].unsqueeze(3).broadcast_to([P, CH, NHEADS, HEADDIM]),
                                      ALU.mult).then_inc(b_xdt, 1)
                    dve.wait_ge(b_G, BW * w + j + 1)
                    dve.tensor_tensor(gm[:, j % 2].rearrange("p a l -> p (a l)"), bank[1][:, 0:3 * P],
                                      causal[:].rearrange("p a l -> p (a l)"), ALU.mult).then_inc(b_gm, 1)
                    advance(side, 2)
                    dve.wait_ge(b_gm, BW * w + j + 1)
                    dve.wait_ge(b_decay, 8 * (BW * w + j + 1))
                    dec, mixed = decay_view(decay[:, j % 2, :]), decay_view(mix[:, j % 2, :])
                    g = gm[:, j % 2].rearrange("p a l -> p (a l)")
                    for part, cols in ((0, slice(0, SEQ)), (1, slice(SEQ, 3 * P))):
                        n = cols.stop - cols.start
                        dve.scalar_tensor_tensor(mixed[part], dec[part], 1.0,
                                                 g[:, cols].unsqueeze(1).broadcast_to([P, NHEADS, n]),
                                                 ALU.min, ALU.mult).then_inc(b_mix, 1)
                    advance(side, 4)

                def gated(j):
                    dve.wait_ge(b_Y, BW * w + j + 1)
                    wait_past(dve, b_O, BW * w + j - 1)
                    for m in range(2):
                        t = slice(SEQ * j, SEQ * j + SEQ)
                        ch.mark(dve.scalar_tensor_tensor(yz[:, j % 2, m, :], xbc[:, m, t], dskip_sb[:, m:m + 1],
                                                         bank[2 + j % 2][:, SEQ * m:SEQ * m + SEQ], ALU.mult, ALU.add))
                    advance(side, 2)
                    ch.settle()
                    dve.tensor_tensor(yz[:, j % 2], yz[:, j % 2], zs[:, :, SEQ * j:SEQ * j + SEQ],
                                      ALU.mult).then_inc(b_yz, 1)
                    advance(side, 2)

                def squares(j):
                    dve.wait_ge(b_sq, BW * w + j + 1)
                    dve.tensor_tensor(ss[:, j % 2, :], sq[:, j % 2, 0, :], sq[:, j % 2, 1, :],
                                      ALU.add).then_inc(b_ss, 1)
                    advance(side, 2)

                def last_norm():
                    dve.wait_ge(b_o, BW * (w + 1))
                    sums = o_sb[:, :, 2 * D:].rearrange("p j (c e) -> p j c e", c=CH)[:, :, :, 0]
                    yield from ch.link(dve.tensor_scalar(fin_v[:].rearrange("p (j c) -> p j c", j=BW), sums,
                                                         1.0 / D_INNER, EPS, ALU.mult, ALU.add))
                    yield from rsqrt(ch, fin)
                    y = fin_y[:].bitcast(F32)
                    for i in range(TW):
                        dve.scalar_tensor_tensor(x_tile(w, i), o_sb[:, i // CH, D * (i % CH):D * (i % CH) + D],
                                                 y[:, i:i + 1], x_tile(w, i), ALU.mult, ALU.add).then_inc(b_x, 1)
                    dve.wait_ge(b_x, TW * (w + 1))
                    step_past(dve, dve_past)

                ch = Chain(dve, b_chain, w * SCAN_STEPS)
                dve.wait_ge(p_zs, 4 * (w + 1))
                weights(0)
                for j in range(BW):
                    if j + 1 < BW:
                        weights(j + 1)
                    gated(j)
                    squares(j)
                for _ in last_norm():
                    advance(side)
                assert ch.k == SCAN_STEPS, ch.k
                finish(side)

            def step(k):
                idle = iter(range(2 * TW))
                late = combine(k - 2, 1) if has(k - 2) else idle
                side = route(k - 1, 1, late) if has(k - 1) else late
                if has(k + 1):
                    experts(k + 1, 0, (count(k + 1), count(k - 1)), side)
                finish(side)
                idle = iter(range(2 * TW))
                late = combine(k + 1, 0) if has(k + 1) else idle
                side = route(k + 2, 0, late) if has(k + 2) else late
                if has(k):
                    mixer(k, side)
                finish(side)
                side = prepare(k + 1) if has(k + 1) else iter(())
                if has(k - 1):
                    experts(k - 1, 1, (count(k + 2), count(k - 1)), side)
                finish(side)

            run_steps(dve, step)


def kernel(**inputs):
    import numpy as np
    import concourse.bacc as bacc
    from concourse.bass_utils import run_bass_kernel_spmd

    def col(v, m):
        v = np.asarray(v)
        return np.ascontiguousarray(np.moveaxis(v.reshape(m, P, *v.shape[1:]), 0, 1))

    a = {k.removeprefix("L0_"): np.asarray(v) for k, v in inputs.items()}
    arrays = {
        "x": a["attn_x"], "w_in_t": np.ascontiguousarray(a["attn_W_in"].T),
        "conv_w": col(a["attn_conv_w"], 4), "conv_b": col(a["attn_conv_b"], 4),
        "dt_bias": a["attn_dt_bias"], "a_log": a["attn_A_log"], "dskip": np.ascontiguousarray(a["attn_Dskip"].reshape(2, 2).T),
        "norm_w": col(a["attn_norm_w"], 2), "w_out_t": np.ascontiguousarray(a["attn_W_out"].T),
        "ln_g": a["attn_ln_g"].reshape(P, 1), "ln_b": a["attn_ln_b"].reshape(P, 1),
        "wr": a["ffn_Wr"], "br": a["ffn_br"], "w1": a["ffn_W1"],
        "b1": np.ascontiguousarray(a["ffn_b1"].reshape(NEXP, 2, P).transpose(2, 0, 1)),
        "w2": a["ffn_W2"], "b2": a["ffn_b2"],
    }
    nc = bacc.Bacc("TRN2", target_bir_lowering=False, num_devices=1)
    args = {n: nc.dram_tensor(f"in_{n}", v.shape, mybir.dt.from_np(v.dtype), kind="ExternalInput").ap()
            for n, v in arrays.items()}
    out = nc.dram_tensor("out", a["attn_x"].shape, F32, kind="ExternalOutput").ap()
    build_program(nc, out=out, **args)
    result = run_bass_kernel_spmd(nc, [{f"in_{n}": v for n, v in arrays.items()}], core_ids=[0])
    return result.results[0]["out"]
```

```python
from contextlib import ExitStack
from itertools import chain

import concourse.bass as bass
from concourse import mybir

ALU = mybir.AluOpType
ACT = mybir.ActivationFunctionType
AX = mybir.AxisListType
F32 = mybir.dt.float32
BF16 = mybir.dt.bfloat16
I32 = mybir.dt.int32
ENGINE = mybir.EngineType

P = 128
D = 128
D_INNER = 256
NHEADS = 4
HEADDIM = D_INNER // NHEADS
NSTATE = 128
D_CONV = 4
NEXP = 8
FF = 256
EPS = 1e-5

SEQ = 256
CH = SEQ // P
BW = 4
TW = BW * CH
ROWS_BOUND = (2 * TW * P + NEXP * (P - 1)) // P
GROUP = 4
IN_FLIGHT = 3
RING = GROUP * IN_FLIGHT
NB = -(-ROWS_BOUND // RING) * RING
GROUPS = NB // GROUP
ROUNDS = NB // RING
ZCOL, XCOL, DTCOL = 0, D_INNER, 2 * D_INNER + 2 * NSTATE
NPROJ = DTCOL + NHEADS
MAGIC = 0x5F3759DF
HUGE = 3.0e38


class Chain:

    def __init__(self, eng, sem, base):
        self.eng, self.sem, self.base, self.k = eng, sem, base, 0

    def mark(self, ins):
        ins.then_inc(self.sem, 1)
        self.k += 1

    def settle(self):
        self.eng.wait_ge(self.sem, self.base + self.k)

    def link(self, ins):
        self.mark(ins)
        yield
        self.settle()


def advance(side, pieces=1):
    for _ in range(pieces):
        next(side, None)


def alternate(a, b):
    live = [a, b]
    while live:
        for chain_ in list(live):
            if next(chain_, live) is live:
                live.remove(chain_)
            else:
                yield


def finish(side):
    for _ in side:
        pass


RSQRT_STEPS = 12
DISPATCH_STEPS = 2 * TW + 1 + RSQRT_STEPS + 30
MIX0_STEPS = 3 * TW + 2 * RSQRT_STEPS + 17
SCAN_STEPS = 2 * BW + 1 + RSQRT_STEPS
COMBINE_STEPS = TW


def build_program(nc, x, w_in_t, conv_w, conv_b, dt_bias, a_log, dskip, norm_w, w_out_t,
                  ln_g, ln_b, wr, br, w1, b1, w2, b2, out):
    n_seq = x.shape[0]
    NT = n_seq * SEQ // P
    NW = NT // TW
    assert NT == NW * TW and NW > 4

    x_rows = x.rearrange("b (c p) d -> p (b c) d", p=P)
    out_rows = out.rearrange("b (c p) d -> p (b c) d", p=P)
    sorted_in = [nc.dram_tensor(f"sorted_in{p}", [NB * P, D], F32, kind="Internal").ap() for p in range(2)]
    sorted_out = [nc.dram_tensor(f"sorted_out{p}", [NB * P, D], F32, kind="Internal").ap() for p in range(2)]
    w1_dram = nc.dram_tensor("w1_dram", [NEXP, P, FF + 2], F32, kind="Internal").ap()
    cs_dram = nc.dram_tensor("cs_rows", [CH * BW * NHEADS, P], F32, kind="Internal").ap()

    with ExitStack() as ctx:
        def sb(name, shape, dt=F32):
            return ctx.enter_context(nc.sbuf_tensor(name, shape, dt))

        def sem(name):
            return ctx.enter_context(nc.semaphore(name))

        ident = sb("ident", [P, P])
        upper = sb("upper", [P, P])
        below_bf = sb("below_bf", [P, P], BF16)
        ones = sb("ones", [P, P])
        ones_bf = sb("ones_bf", [P, P], BF16)
        causal = sb("causal", [P, 3, P])
        expert_rev = sb("expert_rev", [P, TW, NEXP])
        tile_start = sb("tile_start", [P, NEXP, TW])
        block_no = sb("block_no", [1, NB, NEXP])
        not_first = sb("not_first", [P, NEXP, TW])
        itmp = sb("itmp", [P, NB * NEXP], I32)
        w_in_sb = sb("w_in_sb", [P, NPROJ])
        w_out_sb = sb("w_out_sb", [P, 2, D])
        conv_w_sb = sb("conv_w_sb", [P, 4, D_CONV])
        conv_b_sb = sb("conv_b_sb", [P, 4])
        dtb_sb = sb("dtb_sb", [P, NHEADS])
        aneg_sb = sb("aneg_sb", [P, NHEADS])
        dskip_sb = sb("dskip_sb", [P, 2])
        normw_sb = sb("normw_sb", [P, 2])
        lng_sb = sb("lng_sb", [P, 1])
        lnb_sb = sb("lnb_sb", [P, 1])
        wr_pad = sb("wr_pad", [P, 64])
        br_sb = sb("br_sb", [P, NEXP])
        w2_sb = sb("w2_sb", [P, 2 * NEXP, D])
        b2_part = [sb(f"b2_part{i}", [1, NEXP * D], BF16) for i in range(3)]
        b2_parts = sb("b2_parts", [3, NEXP, D], BF16)

        X = sb("X", [P, NT, D])
        stats = sb("stats", [P, TW, 6])
        mv = sb("mv", [P, TW, 2])
        rs_v = sb("rs_v", [P, TW])
        rs_i = sb("rs_i", [P, TW], I32)
        rs_h = sb("rs_h", [P, TW])
        rs_t = sb("rs_t", [P, TW])
        rs_y = sb("rs_y", [P, TW], I32)
        mix_stats = sb("mix_stats", [P, TW, 6])
        mix_mv = sb("mix_mv", [P, TW, 2])
        mix_v = sb("mix_v", [P, TW])
        mix_i = sb("mix_i", [P, TW], I32)
        mix_h = sb("mix_h", [P, TW])
        mix_t = sb("mix_t", [P, TW])
        mix_y = sb("mix_y", [P, TW], I32)
        fin_v = sb("fin_v", [P, TW])
        fin_i = sb("fin_i", [P, TW], I32)
        fin_h = sb("fin_h", [P, TW])
        fin_t = sb("fin_t", [P, TW])
        fin_y = sb("fin_y", [P, TW], I32)
        xn = sb("xn", [P, 2, TW, D])
        xnT = sb("xnT", [P, TW * P])
        lg = sb("lg", [P, TW, NEXP])
        lg2 = sb("lg2", [P, TW, NEXP])
        sc = sb("sc", [P, TW, NEXP])
        oh = sb("oh", [P, 2, TW, NEXP])
        chosen = sb("chosen", [P, TW, NEXP], BF16)
        mx = sb("mx", [P, 4, TW])
        dm = sb("dm", [P, TW])
        ex = sb("ex", [P, TW])
        incl = sb("incl", [P, NEXP, TW])
        rank = sb("rank", [P, NEXP, TW])
        cmp = sb("cmp", [P, NEXP, TW])
        nblk = sb("nblk", [P, NEXP])
        bend = sb("bend", [P, NEXP])
        bstart = sb("bstart", [P, NEXP])
        bcmp = sb("bcmp", [1, NB, NEXP])
        bsum = sb("bsum", [1, NB])
        pos = sb("pos", [P, 2, TW])
        idx = sb("idx", [P, 2, 2, TW], I32)
        gate = sb("gate", [P, 2, 2, TW])
        block_expert = sb("block_expert", [1, 2, NB], I32)

        xb = sb("xb", [P, RING, D])
        w1b = sb("w1b", [P, RING, FF + 2])
        xbT = sb("xbT", [P, 2, P])
        hb = sb("hb", [P, 2, 2, P])
        yb = sb("yb", [P, RING, D])
        yg = sb("yg", [P, 2, TW, D])

        un = sb("un", [P, TW, D])
        unT = sb("unT", [P, TW * P])
        r1 = sb("r1", [P, TW])
        dtx = sb("dtx", [P, CH, BW, NHEADS])
        dta = sb("dta", [P, CH, BW, NHEADS])
        dte = sb("dte", [P, CH, BW, NHEADS])
        dtu = sb("dtu", [P, CH, BW, NHEADS])
        dtl = sb("dtl", [P, CH, BW, NHEADS])
        dtr = sb("dtr", [P, CH, BW, NHEADS])
        dt_t = sb("dt_t", [P, CH, BW, NHEADS])
        a_t = sb("a_t", [P, CH, BW, NHEADS])
        cs_t = sb("cs_t", [P, CH * BW * NHEADS])
        ncs_t = sb("ncs_t", [P, CH, BW, NHEADS])
        cs_r = sb("cs_r", [CH * BW * NHEADS, P])
        csb = sb("csb", [P, CH, BW * NHEADS, P])
        acc = sb("acc", [P, 3, 2 * SEQ])
        xbc = sb("xbc", [P, 4, BW * SEQ])
        zs = sb("zs", [P, 2, BW * SEQ])
        xdt = sb("xdt", [P, 2, CH, NHEADS, HEADDIM])
        gm = sb("gm", [P, 2, 3, P])
        decay = sb("decay", [P, 2, 3 * NHEADS * P])
        w1_whole = decay[:].rearrange("p j a -> p (j a)")[:, 0:NEXP * (FF + 2)].rearrange("p (e f) -> p e f", e=NEXP)
        w1_rows, w1_bias = w1_whole[:, :, 0:FF], w1_whole[:, :, FF:FF + 2]
        b2_row, b2_rest = (zs[0:1, i, 0:NEXP * D] for i in range(2))
        yz = sb("yz", [P, 2, 2, SEQ])
        sq = sb("sq", [P, 2, 2, SEQ])
        o_sb = sb("o_sb", [P, BW, 2 * D + 2 * 64])

        bank = [ctx.enter_context(nc.psum_tensor(f"bank{i}", [P, 512], F32)) for i in range(8)]

        def per_slot(name):
            return [sem(f"{name}_slot{p}") for p in range(2)]

        def per_group(name):
            return [[sem(f"{name}_slot{p}_group{s}") for s in range(IN_FLIGHT)] for p in range(2)]

        router_loaded = sem("router_loaded")
        weights_loaded = sem("weights_loaded")
        pool_consts = sem("pool_consts")
        pool_fill = sem("pool_fill")
        sorted_zeroed = per_slot("sorted_zeroed")
        fixed_dve = sem("fixed_dve")
        fixed_act = sem("fixed_act")
        b2_split = sem("b2_split")
        w1_stored = sem("w1_stored")
        b2_ready = sem("b2_ready")
        sp_past = sem("sp_past")
        pool_past = sem("pool_past")
        dve_past = sem("dve_past")
        x_loaded = sem("x_loaded")
        d_chain = per_slot("d_chain")
        d_xn = per_slot("d_xn")
        d_T = per_slot("d_T")
        d_xT = per_slot("d_xT")
        d_logits = per_slot("d_logits")
        d_margin = per_slot("d_margin")
        d_exp = per_slot("d_exp")
        d_chosen = per_slot("d_chosen")
        d_rank = per_slot("d_rank")
        d_plan = per_slot("d_plan")
        scattered = per_slot("scattered")
        w1_loaded = per_group("w1_loaded")
        xb_loaded = per_group("xb_loaded")
        y_stored = per_group("y_stored")
        e_T = per_slot("e_T")
        e_xT = per_slot("e_xT")
        e_H = per_slot("e_H")
        e_h = per_slot("e_h")
        e_Y = per_slot("e_Y")
        e_y = per_slot("e_y")
        gathered = per_slot("gathered")
        c_chain = per_slot("c_chain")
        c_x = per_slot("c_x")
        out_stored = sem("out_stored")
        m_chain = sem("m_chain")
        m_u = sem("m_u")
        m_T = sem("m_T")
        m_uT = sem("m_uT")
        m_dt = sem("m_dt")
        m_abs = sem("m_abs")
        m_exp = sem("m_exp")
        m_one = sem("m_one")
        m_log = sem("m_log")
        m_a = sem("m_a")
        m_cs = sem("m_cs")
        m_cst = sem("m_cst")
        m_csT = sem("m_csT")
        m_csr = sem("m_csr")
        cs_stored = sem("cs_stored")
        cs_loaded = sem("cs_loaded")
        p_xbc = sem("p_xbc")
        p_z = sem("p_z")
        p_acc = sem("p_acc")
        p_older = sem("p_older")
        p_tap = sem("p_tap")
        p_silu = sem("p_silu")
        p_zs = sem("p_zs")
        b_chain = sem("b_chain")
        b_T = sem("b_T")
        b_G = sem("b_G")
        b_xdt = sem("b_xdt")
        b_gm = sem("b_gm")
        b_decay = sem("b_decay")
        b_mix = sem("b_mix")
        b_Y = sem("b_Y")
        b_yz = sem("b_yz")
        b_sq = sem("b_sq")
        b_O = sem("b_O")
        b_o = sem("b_o")
        b_x = sem("b_x")

        WEIGHT_DMAS = 15
        POOL_CONSTS = 10

        def router_ready(eng):
            eng.wait_ge(router_loaded, 16 * 2)
            eng.wait_ge(pool_consts, POOL_CONSTS)

        def consts_ready(eng):
            eng.wait_ge(weights_loaded, 16 * WEIGHT_DMAS)
            eng.wait_ge(pool_consts, POOL_CONSTS)
            eng.wait_ge(fixed_dve, 3)
            eng.wait_ge(fixed_act, 1)

        def step_past(eng, marker):
            eng.sem_inc(marker, 1)

        def expert_of(eng, p, b):
            return nc.values_load(block_expert[0:1, p, b:b + 1], engines=[eng], min_val=0, max_val=NEXP - 1,
                                  skip_runtime_bounds_check_because="the routing's minimum keeps it in 0 to NEXP - 1")

        T_BANKS, H_BANKS, Y_BANKS = ((0,), (0, 1)), (2, 3), ((4,), (4, 5))
        PROJECT_BANKS = (1, 5, 7)
        PROJECT_TILES = [("xBC", i, q) for q in range(2) for i in range(4)] + [("z", m, q) for q in range(2) for m in range(2)]

        def decay_view(s):
            first = s[:, 0:NHEADS * SEQ].rearrange("p (h l) -> p h l", h=NHEADS)
            second = s[:, NHEADS * SEQ:].rearrange("p (h l) -> p h l", h=NHEADS)
            return first, second

        LOOP_FROM, LOOP_TO = 2, NW - 2

        def has(v):
            return not isinstance(v, int) or 0 <= v < NW

        def served(v, p):
            if isinstance(v, int):
                return min(v + 1, NW - 1) if p == 0 else max(v - 1, 0)
            return v + 1 if p == 0 else v - 1

        def wait_past(eng, semaphore, value):
            if not isinstance(value, int) or value > 0:
                eng.wait_ge(semaphore, value)

        def run_steps(eng, first_steps, step, last_steps):
            first_steps()
            for k in range(1, LOOP_FROM):
                step(k)
            with eng.Fori(LOOP_FROM, LOOP_TO) as k:
                step(k)
            for k in range(LOOP_TO, NW - 1):
                step(k)
            last_steps()

        block = ctx.enter_context(nc.Block())

        @block.sync
        def _(sp):
            def load_x(v):
                sp.dma_start(X[:, bass.ds(v * TW, TW), :], x_rows[:, bass.ds(v * TW, TW), :]).then_inc(x_loaded, 16)

            load_x(0)
            sp.wait_ge(pool_fill, 1)
            sp.dma_start(wr_pad[:, 0:NEXP], wr).then_inc(router_loaded, 16)
            sp.dma_start(br_sb[:], br.partition_broadcast(P)).then_inc(router_loaded, 16)
            loads = [
                (w1_rows, w1.rearrange("e h f -> h e f")), (w1_bias, b1),
                (b2_row, b2.rearrange("e d -> (e d)").unsqueeze(0)),
                (lng_sb[:], ln_g), (lnb_sb[:], ln_b),
                (dtb_sb[:], dt_bias.partition_broadcast(P)), (aneg_sb[:], a_log.partition_broadcast(P)),
                (conv_w_sb[:], conv_w), (conv_b_sb[:], conv_b), (normw_sb[:], norm_w),
                (w2_sb[:], w2.rearrange("e (m p) n -> p (e m) n", p=P)),
                (w_in_sb[:], w_in_t), (w_out_sb[:], w_out_t.rearrange("(m p) n -> p m n", p=P)),
                *((dskip_sb[64 * g:64 * g + 64, :], dskip[g].partition_broadcast(64)) for g in range(2)),
            ]
            assert len(loads) == WEIGHT_DMAS
            for dst, src in loads:
                sp.dma_start(dst, src).then_inc(weights_loaded, 16)
            sp.wait_ge(pool_fill, 2)
            zero = yg[:].rearrange("p k i d -> p (k i) d")
            for p in (1, 0):
                rows = sorted_in[p].rearrange("(k p) d -> p k d", p=P)
                for a in range(0, NB, 2 * TW):
                    k = min(2 * TW, NB - a)
                    sp.dma_start(rows[:, a:a + k, :], zero[:, 0:k, :]).then_inc(sorted_zeroed[p], 16)
            sp.wait_ge(weights_loaded, 16 * WEIGHT_DMAS)
            sp.dma_start(w1_dram.rearrange("e h f -> h e f"), w1_whole).then_inc(w1_stored, 16)
            load_x(1)
            sp.wait_ge(w1_stored, 16)
            sp.wait_ge(b2_split, 5)
            for i in range(3):
                sp.dma_start(b2_parts[i:i + 1].rearrange("p e d -> p (e d)"), b2_part[i][:]).then_inc(b2_ready, 16)

            def wait_sp(semaphore, value):
                wait_past(sp, semaphore, value)
                step_past(sp, sp_past)

            def experts_of(p, g):
                return [expert_of(ENGINE.SP, p, GROUP * g + a) for a in range(GROUP)]

            def rows_of(dram, g):
                return dram[g * GROUP * P:(g + 1) * GROUP * P, :].rearrange("(a p) d -> p a d", p=P)

            def load(p, g, experts):
                s = g % IN_FLIGHT
                sp.dma_start(xb[:, GROUP * s:GROUP * s + GROUP, :], rows_of(sorted_in[p], g)).then_inc(xb_loaded[p][s], 16)
                for a, e in enumerate(experts):
                    sp.dma_start(w1b[:, GROUP * s + a, :], w1_dram[bass.ds(e, 1)].rearrange("a h f -> (a h) f")).then_inc(w1_loaded[p][s], 16)

            def store(v, p, g):
                s = g % IN_FLIGHT
                wait_sp(e_y[p], v * NB + GROUP * (g + 1))
                sp.dma_start(rows_of(sorted_out[p], g), yb[:, GROUP * s:GROUP * s + GROUP, :]).then_inc(y_stored[p][s], 16)

            def sources_ready(v, p):
                wait_sp(d_plan[p], v + 1)
                wait_sp(scattered[p], 256 * (v + 1))

            def first_loads(v, p):
                sources_ready(v, p)
                for g in range(IN_FLIGHT):
                    load(p, g, experts_of(p, g))

            def store_decays(w):
                wait_sp(cs_loaded, 16 * w)
                wait_sp(m_csr, w + 1)
                sp.dma_start(cs_dram, cs_r[:]).then_inc(cs_stored, 16)

            def spread_decays(w):
                wait_sp(cs_stored, 16 * (w + 1))
                sp.dma_start(csb[:].rearrange("p c k l -> p (c k l)"),
                             cs_dram.rearrange("r l -> (r l)").partition_broadcast(P)).then_inc(cs_loaded, 16)

            def store_out(w, p, combines):
                wait_sp(c_x[p], TW * combines)
                sp.dma_start(out_rows[:, bass.ds(w * TW, TW), :],
                             X[:, bass.ds(w * TW, TW), :]).then_inc(out_stored, 16)

            def experts(v, p, next_v, w=None):
                if w is not None:
                    store_decays(w)
                wait_sp(gathered[p], 256 * v)
                coming = experts_of(p, IN_FLIGHT)
                for g in range(GROUPS):
                    ahead = g + IN_FLIGHT
                    if ahead == GROUPS and next_v is not None:
                        sources_ready(next_v, 1 - p)
                        coming = experts_of(1 - p, 0)
                    store(v, p, g)
                    if g == 1 and w is not None:
                        spread_decays(w)
                    if ahead < GROUPS:
                        load(p, ahead, coming)
                        if ahead + 1 < GROUPS:
                            coming = experts_of(p, ahead + 1)
                    elif next_v is not None:
                        load(1 - p, ahead - GROUPS, coming)
                        if ahead + 1 < GROUPS + IN_FLIGHT:
                            coming = experts_of(1 - p, ahead + 1 - GROUPS)

            def step(k):
                if has(k + 1):
                    if not has(k - 2):
                        first_loads(k, 0)
                        load_x(k + 2)
                    experts(k, 0, None, k)
                else:
                    store_decays(k)
                    spread_decays(k)
                if has(k - 2):
                    store_out(k - 2, 1, k)
                if has(k + 3):
                    load_x(k + 3)
                first_loads(k, 1)
                experts(k, 1, k + 1 if has(k + 2) else None)

            first_loads(0, 1)
            experts(0, 1, None)
            wait_sp(d_plan[0], 1)
            load_x(2)
            first_loads(0, 0)
            experts(0, 0, None)
            store_decays(0)
            spread_decays(0)
            for k in range(1, LOOP_FROM):
                step(k)
            with sp.Fori(LOOP_FROM, LOOP_TO - 1) as k:
                step(k)
            for k in range(LOOP_TO - 1, NW):
                step(k)
            first_loads(NW - 1, 0)
            experts(NW - 1, 0, None)
            store_out(NW - 2, 1, NW)
            store_out(NW - 1, 0, NW)
            sp.wait_ge(out_stored, 16 * NW)

        @block.gpsimd
        def _(pool):
            pool.memset(wr_pad[:], 0.0).then_inc(pool_fill, 1)
            pool.memset(yg[:], 0.0).then_inc(pool_fill, 1)
            pool.memset(ident[:], 0.0).then_inc(pool_consts, 1)
            pool.memset(ones[:], 1.0).then_inc(pool_consts, 1)
            pool.memset(ones_bf[:], 1.0).then_inc(pool_consts, 1)
            pool.memset(causal[:, 1, :], 1.0).then_inc(pool_consts, 1)
            pool.wait_ge(pool_consts, 4)
            pool.affine_select(out=ident[:], in_=ident[:], compare_op=ALU.not_equal, fill=1.0, base=0,
                               pattern=[[-1, P]], channel_multiplier=1).then_inc(pool_consts, 1)
            for dst in (upper[:], causal[:, 0, :], causal[:, 2, :]):
                pool.affine_select(out=dst, in_=ones[:], compare_op=ALU.is_ge, fill=0.0, base=0,
                                   pattern=[[1, P]], channel_multiplier=-1).then_inc(pool_consts, 1)
            pool.affine_select(out=below_bf[:], in_=ones_bf[:], compare_op=ALU.is_ge, fill=0.0, base=-1,
                               pattern=[[1, P]], channel_multiplier=-1).then_inc(pool_consts, 1)

            def numbers(dst, parts, base, pattern, n):
                if n:
                    pool.wait_ge(pool_fill, 2 + 2 * n)
                pool.iota(itmp[0:parts, 0:dst.free_size()], pattern=pattern, base=base,
                          channel_multiplier=0).then_inc(pool_fill, 1)
                pool.wait_ge(pool_fill, 3 + 2 * n)
                pool.tensor_copy(dst, itmp[0:parts, 0:dst.free_size()]).then_inc(pool_fill, 1)

            numbers(expert_rev[:].rearrange("p i e -> p (i e)"), P, NEXP, [[0, TW], [-1, NEXP]], 0)
            numbers(tile_start[:].rearrange("p e j -> p (e j)"), P, 0, [[0, NEXP], [P, TW]], 1)
            numbers(block_no[:].rearrange("p k e -> p (k e)"), 1, 0, [[1, NB], [0, NEXP]], 2)
            pool.memset(not_first[:], 1.0).then_inc(pool_fill, 1)
            pool.wait_ge(pool_fill, 9)
            pool.memset(not_first[:, :, 0:1], 0.0).then_inc(pool_consts, 1)

            def scatter(v, p):
                pool.wait_ge(d_plan[p], v + 1)
                pool.wait_ge(sorted_zeroed[p], 16 * -(-NB // (2 * TW)))
                wait_past(pool, e_T[p], v * NB)
                step_past(pool, pool_past)
                for k in range(2):
                    for i in range(TW):
                        pool.indirect_dma_start(
                            out=sorted_in[p], out_offset=bass.IndirectOffsetOnAxis(ap=idx[:, p, k, i:i + 1], axis=0),
                            in_=xn[:, p, i, :], in_offset=None).then_inc(scattered[p], 16)

            def gather(v, p, other):
                for s in range(IN_FLIGHT):
                    pool.wait_ge(y_stored[p][s], 16 * ROUNDS * (v + 1))
                wait_past(pool, c_x[p], TW * v)
                wait_past(pool, c_x[1 - p], TW * other)
                step_past(pool, pool_past)
                for k in range(2):
                    for i in range(TW):
                        pool.indirect_dma_start(
                            out=yg[:, k, i, :], out_offset=None, in_=sorted_out[p],
                            in_offset=bass.IndirectOffsetOnAxis(ap=idx[:, p, k, i:i + 1], axis=0)).then_inc(gathered[p], 16)

            def step(k):
                if has(k - 2):
                    gather(k - 1, 1, k)
                scatter(k, 1)
                gather(k, 0, k)
                if has(k + 2):
                    scatter(k + 1, 0)

            def first_steps():
                scatter(0, 1)
                scatter(0, 0)
                gather(0, 1, 0)
                gather(0, 0, 1)
                scatter(1, 0)

            def last_steps():
                k = NW - 1
                gather(k - 1, 1, k)
                scatter(k, 1)
                scatter(k, 0)
                gather(k, 1, k)
                gather(k, 0, NW)

            run_steps(pool, first_steps, step, last_steps)

        @block.scalar
        def _(act):
            def route(v, p):
                for half in range(2):
                    act.wait_ge(d_T[p], 2 * v + half + 1)
                    act.activation(xnT[:, 512 * half:512 * half + 512], bank[6][:], ACT.Copy).then_inc(d_xT[p], 1)
                    yield
                act.wait_ge(d_margin[p], v + 1)
                act.activation(ex[:], dm[:], ACT.Exp).then_inc(d_exp[p], 1)
                yield

            def prepare(v):
                for half in range(2):
                    act.wait_ge(m_T, 2 * v + half + 1)
                    act.activation(unT[:, 512 * half:512 * half + 512], bank[6][:], ACT.Identity,
                                   bias=lnb_sb[:], scale=lng_sb[:]).then_inc(m_uT, 1)
                    yield
                act.wait_ge(m_abs, v + 1)
                act.activation(dte[:], dta[:], ACT.Exp, scale=-1.0).then_inc(m_exp, 1)
                yield
                act.wait_ge(m_one, v + 1)
                act.activation(dtl[:], dtu[:], ACT.Ln).then_inc(m_log, 1)
                yield
                act.wait_ge(m_csT, v + 1)
                wait_past(act, cs_stored, 16 * v)
                act.activation(cs_r[:], bank[7][0:CH * BW * NHEADS, 0:P], ACT.Copy).then_inc(m_csr, 1)

            def experts(v, p, done, side, at, second=iter(()), second_at=()):
                for q in range(2):
                    wait_past(act, e_Y[q], NB * done[q])

                def take_x(b):
                    act.wait_ge(e_T[p], v * NB + b + 1)
                    if b >= 2:
                        act.wait_ge(e_H[p], v * NB + b - 1)
                    act.activation(xbT[:, b % 2, :], bank[T_BANKS[p][b % len(T_BANKS[p])]][:, 0:P],
                                   ACT.Copy).then_inc(e_xT[p], 1)

                def hidden(b):
                    act.wait_ge(e_H[p], v * NB + b + 1)
                    if b >= 2:
                        act.wait_ge(e_Y[p], v * NB + b - 1)
                    for f in range(2):
                        ins = act.activation(hb[:, b % 2, f, :], bank[H_BANKS[b % 2]][:, P * f:P * f + P], ACT.Relu,
                                             bias=w1b[:, b % RING, FF + f:FF + f + 1])
                    ins.then_inc(e_h[p], 1)

                take_x(0)
                for b in range(NB):
                    if b + 1 < NB:
                        take_x(b + 1)
                    hidden(b)
                    advance(side, at.count(b))
                    advance(second, second_at.count(b))
                finish(second)
                finish(side)

            def project(w):
                def newest(k):
                    act.wait_ge(p_xbc, 8 * w + k + 1)
                    if k >= 3:
                        act.wait_ge(p_silu, 8 * w + k - 2)
                    i = k % 4
                    act.activation(acc[:, k % 3, :], bank[PROJECT_BANKS[k % 3]][:], ACT.Identity,
                                   bias=conv_b_sb[:, i:i + 1],
                                   scale=conv_w_sb[:, i, D_CONV - 1:D_CONV]).then_inc(p_acc, 1)

                def silu(k):
                    act.wait_ge(p_tap, 8 * w + k + 1)
                    act.activation(xbc[:, k % 4, 512 * (k // 4):512 * (k // 4) + 512], acc[:, k % 3, :],
                                   ACT.Silu).then_inc(p_silu, 1)

                def gate_of(n):
                    m, q = n % 2, n // 2
                    act.wait_ge(p_z, 4 * w + n + 1)
                    act.activation(zs[:, m, 512 * q:512 * q + 512], bank[PROJECT_BANKS[(8 + n) % 3]][:],
                                   ACT.Silu).then_inc(p_zs, 1)

                for k in range(8):
                    newest(k)
                    yield
                    if k >= 2:
                        silu(k - 2)
                        yield
                for piece, n in ((gate_of, 0), (silu, 6), (gate_of, 1), (silu, 7), (gate_of, 2), (gate_of, 3)):
                    piece(n)
                    yield

            def mixer(w, side):
                def decays(j):
                    if j == 0:
                        act.wait_ge(cs_loaded, 16 * (w + 1))
                    wait_past(act, b_Y, BW * w + j - 1)
                    first, second = decay_view(decay[:, j % 2, :])
                    for h in range(NHEADS):
                        act.activation(first[:, h, :].rearrange("p (c l) -> p c l", c=CH),
                                       csb[:, :, j * NHEADS + h, :], ACT.Exp,
                                       bias=ncs_t[:, 0, j, h:h + 1]).then_inc(b_decay, 1)
                    for h in range(NHEADS):
                        act.activation(second[:, h, :], csb[:, 1, j * NHEADS + h, :], ACT.Exp,
                                       bias=ncs_t[:, 1, j, h:h + 1]).then_inc(b_decay, 1)

                def square(j):
                    act.wait_ge(b_yz, BW * w + j + 1)
                    wait_past(act, b_O, BW * w + j - 1)
                    act.activation(sq[:, j % 2], yz[:, j % 2], ACT.Square).then_inc(b_sq, 1)

                def take_out(j):
                    act.wait_ge(b_O, BW * w + j + 1)
                    act.activation(o_sb[:, j, :], bank[4 + j % 2][:, 0:2 * D + 2 * 64], ACT.Copy).then_inc(b_o, 1)

                advance(side)
                decays(0)
                advance(side)
                wait_past(act, b_x, TW * w)
                for j in range(BW):
                    if j + 1 < BW:
                        decays(j + 1)
                    square(j)
                    if j >= 1:
                        take_out(j - 1)
                take_out(BW - 1)

            def step(k):
                experts(k, 0, (k, k), route(k, 1), ROUTE_AT, project(k), PROJECT_AT)
                side = route(k + 1, 0) if has(k + 2) else iter(range(3))
                mixer(k, side)
                experts(k, 1, (k + 1, k), chain(side, prepare(k + 1)), PREPARE_AT)

            def first_steps():
                finish(route(0, 1))
                act.wait_ge(weights_loaded, 16 * WEIGHT_DMAS)
                act.activation(aneg_sb[:], aneg_sb[:], ACT.Exp).then_inc(fixed_act, 1)
                consts_ready(act)
                experts(0, 1, (0, 0), route(0, 0), (3, 4, 6))
                experts(0, 0, (0, 1), route(1, 0), (3, 4, 6))
                finish(prepare(0))
                finish(project(0))
                mixer(0, iter(range(3)))
                finish(prepare(1))

            ROUTE_AT = (11, 13, 22)
            PROJECT_AT = (1, 3) + tuple(range(5, 23))
            PREPARE_AT = (1, 15, 17, 19, 20, 22)

            def last_steps():
                k = NW - 1
                finish(project(k))
                finish(route(k, 1))
                mixer(k, iter(range(3)))
                experts(k, 1, (k, k), route(k, 0), (3, 4, 6))
                experts(k, 0, (k, NW), iter(()), ())

            run_steps(act, first_steps, step, last_steps)

        @block.tensor
        def _(pe):
            def small_banks_free(plans0, plans1, prepared):
                wait_past(pe, d_plan[0], plans0)
                wait_past(pe, d_plan[1], plans1)
                wait_past(pe, m_chain, prepared * MIX0_STEPS)
                wait_past(pe, m_csr, prepared)

            def route(v, p, used):
                small_banks_free(*used)
                for half in range(2):
                    if half == 1:
                        pe.wait_ge(d_xT[p], 2 * v + 1)
                    pe.wait_ge(d_xn[p], TW * v + 4 * half + 4)
                    for i in range(4):
                        mm = pe.transpose(bank[6][:, P * i:P * i + P], xn[:, p, 4 * half + i, :], ident[:])
                    mm.then_inc(d_T[p], 1)
                    yield
                pe.wait_ge(d_xT[p], 2 * v + 2)
                for i in range(TW):
                    mm = pe.matmul(bank[6][:, 64 * i:64 * i + 64], xnT[:, P * i:P * i + P], wr_pad[:],
                                   start=True, stop=True)
                mm.then_inc(d_logits[p], 1)
                yield
                pe.wait_ge(d_chosen[p], v + 1)
                by_expert = chosen[:].rearrange("p i e -> p e i")
                pe.matmul(bank[6][:, 0:64], below_bf[:], by_expert, start=True, stop=True)
                pe.matmul(bank[6][:, 64:128], ones_bf[:], by_expert, start=True, stop=True).then_inc(d_rank[p], 1)
                yield

            def prepare(v, used):
                small_banks_free(*used)
                for half in range(2):
                    pe.wait_ge(m_u, TW * v + 4 * half + 4)
                    if half == 1:
                        pe.wait_ge(m_uT, 2 * v + 1)
                    for i in range(4):
                        mm = pe.transpose(bank[6][:, P * i:P * i + P], un[:, 4 * half + i, :], ident[:])
                    mm.then_inc(m_T, 1)
                    yield
                pe.wait_ge(m_uT, 2 * v + 2)
                for i in range(TW):
                    mm = pe.matmul(bank[7][:, 64 * i:64 * i + 64], unT[:, P * i:P * i + P],
                                   w_in_sb[:, NPROJ - 64:NPROJ], start=True, stop=True)
                mm.then_inc(m_dt, 1)
                yield
                pe.wait_ge(m_a, v + 1)
                half = BW * NHEADS
                a_rows = a_t[:].rearrange("p c j h -> p (c j h)")
                pe.matmul(bank[6][:, 0:2 * half], upper[:], a_rows, start=True, stop=False)
                pe.matmul(bank[6][:, half:2 * half], ones[:], a_rows[:, 0:half], start=False,
                          stop=True).then_inc(m_cs, 1)
                yield
                pe.wait_ge(m_cst, v + 1)
                pe.transpose(bank[7][0:2 * half, 0:P], cs_t[:], ident[:]).then_inc(m_csT, 1)

            def banks_free(done):
                for q in range(2):
                    wait_past(pe, e_y[q], NB * done[q])
                wait_past(pe, b_o, BW * done[2])

            def experts(v, p, done, side, at, second=iter(()), second_at=()):
                t_banks, y_banks = T_BANKS[p], Y_BANKS[p]
                pe.wait_ge(d_plan[p], v + 1)

                def turn_x(b):
                    if b % GROUP == 0:
                        pe.wait_ge(xb_loaded[p][b % RING // GROUP], 16 * (ROUNDS * v + b // RING + 1))
                    if b >= len(t_banks):
                        pe.wait_ge(e_xT[p], v * NB + b + 1 - len(t_banks))
                    pe.transpose(bank[t_banks[b % len(t_banks)]][:, 0:P], xb[:, b % RING, :], ident[:]).then_inc(e_T[p], 1)

                def up(b):
                    if b % GROUP == 0:
                        pe.wait_ge(w1_loaded[p][b % RING // GROUP], 16 * GROUP * (ROUNDS * v + b // RING + 1))
                    pe.wait_ge(e_xT[p], v * NB + b + 1)
                    if b >= 2:
                        pe.wait_ge(e_h[p], v * NB + b - 1)
                    for f in range(2):
                        mm = pe.matmul(bank[H_BANKS[b % 2]][:, P * f:P * f + P], w1b[:, b % RING, P * f:P * f + P],
                                       xbT[:, b % 2, :], start=True, stop=True)
                        if f == 0:
                            numbers[b % 2] = expert_of(ENGINE.PE, p, b)
                    mm.then_inc(e_H[p], 1)

                def down(b):
                    e = numbers[b % 2]
                    pe.wait_ge(e_h[p], v * NB + b + 1)
                    if b == 0:
                        banks_free(done)
                    if b >= len(y_banks):
                        pe.wait_ge(e_y[p], v * NB + b + 1 - len(y_banks))
                    y = bank[y_banks[b % len(y_banks)]][:, 0:P]
                    pe.matmul(y, ones_bf[0:3, :],
                              b2_parts[:, bass.ds(e, 1), :].rearrange("p a d -> p (a d)"), start=True, stop=False)
                    for f in range(2):
                        mm = pe.matmul(y, hb[:, b % 2, f, :],
                                       w2_sb[:, bass.ds(2 * e + f, 1), :].rearrange("p a d -> p (a d)"),
                                       start=False, stop=(f == 1))
                    mm.then_inc(e_Y[p], 1)

                numbers = [None, None]
                turn_x(0)
                turn_x(1)
                up(0)
                for b in range(NB):
                    if b + 2 < NB:
                        turn_x(b + 2)
                    if b >= 1:
                        down(b - 1)
                    if b + 1 < NB:
                        up(b + 1)
                    advance(side, at.count(b))
                    advance(second, second_at.count(b))
                down(NB - 1)
                finish(second)
                finish(side)

            def project(w, done):
                banks_free(done)
                pe.wait_ge(m_csr, w + 1)
                for n, (what, i, q) in enumerate(PROJECT_TILES):
                    if n >= 3 and PROJECT_TILES[n - 3][0] == "xBC":
                        pe.wait_ge(p_tap, 8 * w + n - 2)
                    elif n >= 3:
                        pe.wait_ge(p_zs, 4 * w + n - 10)
                    first, ready = (XCOL, p_xbc) if what == "xBC" else (ZCOL, p_z)
                    pe.matmul(bank[PROJECT_BANKS[n % 3]][:], w_in_sb[:, first + P * i:first + P * i + P],
                              unT[:, 512 * q:512 * q + 512], start=True, stop=True).then_inc(ready, 1)
                    yield

            def mixer(w, done, side):

                def sources(j):
                    wait_past(pe, b_xdt, BW * w + j)
                    for c in range(CH):
                        for m in range(2):
                            t = SEQ * j + P * c
                            mm = pe.transpose(bank[0][:, 256 * c + P * m:256 * c + P * m + P],
                                              xbc[:, m, t:t + P], ident[:])
                    mm.then_inc(b_T, 1)
                    wait_past(pe, b_gm, BW * w + j)
                    t = SEQ * j
                    pe.matmul(bank[1][:, 0:SEQ], xbc[:, 2, t:t + P], xbc[:, 3, t:t + SEQ], start=True, stop=True)
                    pe.matmul(bank[1][:, SEQ:SEQ + P], xbc[:, 2, t + P:t + SEQ], xbc[:, 3, t + P:t + SEQ],
                              start=True, stop=True).then_inc(b_G, 1)

                def outputs(j):
                    pe.wait_ge(b_mix, 2 * (BW * w + j + 1))
                    wait_past(pe, b_yz, BW * w + j - 1)
                    first, second = decay_view(decay[:, j % 2, :])
                    for h in range(NHEADS):
                        a = HEADDIM * (h % 2)
                        o = bank[2 + j % 2][a:a + HEADDIM, SEQ * (h // 2):SEQ * (h // 2) + SEQ]
                        pe.matmul(o, xdt[:, j % 2, 0, h, :], first[:, h, :], start=True, stop=False)
                        mm = pe.matmul(o[:, P:SEQ], xdt[:, j % 2, 1, h, :], second[:, h, :], start=False, stop=True)
                    mm.then_inc(b_Y, 1)

                def project_out(j):
                    if j == 0:
                        banks_free(done)
                    pe.wait_ge(b_sq, BW * w + j + 1)
                    wait_past(pe, b_o, BW * w + j - 1)
                    o = bank[4 + j % 2]
                    for c in range(CH):
                        for m in range(2):
                            pe.matmul(o[:, D * c:D * c + D], yz[:, j % 2, m, P * c:P * c + P], w_out_sb[:, m, :],
                                      start=(m == 0), stop=(m == 1))
                        for m in range(2):
                            mm = pe.matmul(o[:, 2 * D + 64 * c:2 * D + 64 * c + 64], sq[:, j % 2, m, P * c:P * c + P],
                                           ones[:, 0:64], start=(m == 0), stop=(m == 1))
                    mm.then_inc(b_O, 1)

                pe.wait_ge(p_silu, 8 * (w + 1))
                pe.wait_ge(p_zs, 4 * (w + 1))
                advance(side)
                sources(0)
                advance(side)
                sources(1)
                advance(side)
                outputs(0)
                for j in range(BW):
                    if j + 2 < BW:
                        sources(j + 2)
                    if j + 1 < BW:
                        outputs(j + 1)
                    project_out(j)
                    if j == 1:
                        advance(side)

            def step(k):
                experts(k, 0, (k, k, k), route(k, 1, (k + 1, k, k + 1)), ROUTE_AT, project(k, (k, k, k)), PROJECT_AT)
                side = route(k + 1, 0, (k + 1, k + 1, k + 1)) if has(k + 2) else iter(())
                mixer(k, (k + 1, k, k), side)
                finish(side)
                routed = k + 2 if has(k + 2) else k + 1
                experts(k, 1, (k + 1, k, k + 1), prepare(k + 1, (routed, k + 1, k + 1)), PREPARE_AT)

            def first_steps():
                router_ready(pe)
                finish(route(0, 1, (0, 0, 0)))
                consts_ready(pe)
                pe.wait_ge(b2_ready, 16 * 3)
                experts(0, 1, (0, 0, 0), route(0, 0, (0, 1, 0)), (3, 4, 5, 6))
                experts(0, 0, (0, 1, 0), route(1, 0, (1, 1, 0)), (3, 4, 5, 6))
                finish(prepare(0, (1, 1, 0)))
                finish(project(0, (1, 1, 0)))
                mixer(0, (1, 1, 0), iter(()))
                finish(prepare(1, (2, 1, 1)))

            ROUTE_AT = (10, 12, 14, 19)
            PROJECT_AT = (0, 2, 4, 6, 8, 10, 12, 14, 16, 18, 20, 21)
            PREPARE_AT = (15, 16, 18, 21, 22)

            def last_steps():
                k = NW - 1
                finish(project(k, (k, k, k)))
                finish(route(k, 1, (k, k, NW)))
                mixer(k, (k, k, k), iter(()))
                experts(k, 1, (k, k, NW), route(k, 0, (k, NW, NW)), (3, 4, 5, 6))
                experts(k, 0, (k, NW, NW), iter(()), ())

            run_steps(pe, first_steps, step, last_steps)

        @block.vector
        def _(dve):
            def rsqrt(ch, bufs):
                v, i, h, t, yi = (b[:] for b in bufs)
                y = yi.bitcast(F32)
                yield from ch.link(dve.tensor_scalar(i, v.bitcast(I32), 1, None, ALU.logical_shift_right))
                yield from ch.link(dve.tensor_scalar(yi, i, -1.0, float(MAGIC), ALU.mult, ALU.add))
                yield from ch.link(dve.tensor_scalar(h, v, -0.5, None, ALU.mult))
                for _ in range(3):
                    yield from ch.link(dve.tensor_tensor(t, y, y, ALU.mult))
                    yield from ch.link(dve.tensor_tensor(t, t, h, ALU.mult))
                    yield from ch.link(dve.scalar_tensor_tensor(y, t, 1.5, y, ALU.add, ALU.mult))

            rs = (rs_v, rs_i, rs_h, rs_t, rs_y)
            prep = (mix_v, mix_i, mix_h, mix_t, mix_y)
            fin = (fin_v, fin_i, fin_h, fin_t, fin_y)

            def x_tile(w, i):
                return X[:, bass.ds(w * TW + i, 1), :].rearrange("p a d -> p (a d)")

            def moments(ch, w, stats, mv, var_eps):
                for i in range(TW):
                    ch.mark(dve.bn_stats(stats[:, i, :], x_tile(w, i)))
                    yield
                ch.settle()
                step_past(dve, dve_past)
                for i in range(TW):
                    ch.mark(dve.bn_aggr(mv[:, i, :], stats[:, i, :]))
                    yield
                ch.settle()
                yield from ch.link(dve.tensor_scalar(var_eps[:], mv[:, :, 1], EPS, None, ALU.add))

            def over_experts(a):
                return a.unsqueeze(2).broadcast_to([P, TW, NEXP])

            def route(v, p, other):
                w = served(v, p)
                if p == 0 or isinstance(v, int) and v == 0:
                    dve.wait_ge(x_loaded, 16 * (w + 1))
                    step_past(dve, dve_past)
                ch = Chain(dve, d_chain[p], v * DISPATCH_STEPS)
                stats_, mv_, bufs = (mix_stats, mix_mv, prep) if p == 0 else (stats, mv, rs)
                yield from moments(ch, w, stats_, mv_, bufs[0])
                yield from rsqrt(ch, bufs)
                y = bufs[4][:].bitcast(F32)
                wait_past(dve, scattered[p], 256 * v)
                for i in range(TW):
                    dve.tensor_scalar(xn[:, p, i, :], x_tile(w, i), mv_[:, i, 0:1], y[:, i:i + 1],
                                      ALU.subtract, ALU.mult).then_inc(d_xn[p], 1)
                    yield
                dve.wait_ge(d_logits[p], v + 1)
                logits = bank[6][:].rearrange("p (i e) -> p i e", i=TW)[:, :, 0:NEXP]
                yield from ch.link(dve.tensor_tensor(lg[:], logits, br_sb[:].unsqueeze(1).broadcast_to([P, TW, NEXP]),
                                                     ALU.add))
                src = lg
                for k in range(2):
                    yield from ch.link(dve.tensor_reduce(mx[:, 2 * k, :], src[:], AX.X, ALU.max))
                    yield from ch.link(dve.tensor_tensor(sc[:], src[:], over_experts(mx[:, 2 * k, :]), ALU.is_equal))
                    yield from ch.link(dve.tensor_tensor(sc[:], sc[:], expert_rev[:], ALU.mult))
                    yield from ch.link(dve.tensor_reduce(mx[:, 2 * k + 1, :], sc[:], AX.X, ALU.max))
                    yield from ch.link(dve.tensor_tensor(oh[:, k], expert_rev[:], over_experts(mx[:, 2 * k + 1, :]),
                                                         ALU.is_equal))
                    if k == 0:
                        yield from ch.link(dve.scalar_tensor_tensor(lg2[:], oh[:, 0], -HUGE, lg[:], ALU.mult, ALU.add))
                        src = lg2
                dve.tensor_tensor(chosen[:], oh[:, 0], oh[:, 1], ALU.add).then_inc(d_chosen[p], 1)
                dve.tensor_tensor(dm[:], mx[:, 2, :], mx[:, 0, :], ALU.subtract).then_inc(d_margin[p], 1)
                yield
                def places():
                    dve.wait_ge(d_rank[p], v + 1)
                    before = bank[6][:, 0:64].rearrange("p (e i) -> p e i", e=NEXP)
                    total = bank[6][:, 64:128].rearrange("p (e i) -> p e i", e=NEXP)
                    yield from ch.link(dve.tensor_tensor_scan(incl[:].rearrange("p e i -> p (e i)"),
                                                              not_first[:].rearrange("p e i -> p (e i)"),
                                                              bank[6][:, 64:128], 0.0, ALU.mult, ALU.add))
                    yield from ch.link(dve.tensor_tensor(rank[:], incl[:], total, ALU.subtract))
                    yield from ch.link(dve.tensor_tensor(rank[:], rank[:], before, ALU.add))
                    yield from ch.link(dve.tensor_tensor(cmp[:], incl[:, :, TW - 1:TW].broadcast_to([P, NEXP, TW]),
                                                         tile_start[:], ALU.is_gt))
                    yield from ch.link(dve.tensor_reduce(nblk[:], cmp[:], AX.X, ALU.add))
                    yield from ch.link(dve.tensor_tensor_scan(bend[:], ones[:, 0:NEXP], nblk[:], 0.0, ALU.mult, ALU.add))
                    yield from ch.link(dve.tensor_tensor(bstart[:], bend[:], nblk[:], ALU.subtract))
                    yield from ch.link(dve.scalar_tensor_tensor(rank[:], bstart[:].unsqueeze(2).broadcast_to([P, NEXP, TW]),
                                                                float(P), rank[:], ALU.mult, ALU.add))
                    by_tile = rank[:].rearrange("p e i -> p i e")
                    for k in range(2):
                        yield from ch.link(dve.tensor_tensor(sc[:], oh[:, k], by_tile, ALU.mult))
                        yield from ch.link(dve.tensor_reduce(pos[:, k, :], sc[:], AX.X, ALU.add))
                    yield from ch.link(dve.tensor_tensor(bcmp[:], bend[0:1, :].unsqueeze(1).broadcast_to([1, NB, NEXP]),
                                                         block_no[:], ALU.is_le))
                    yield from ch.link(dve.tensor_reduce(bsum[:], bcmp[:], AX.X, ALU.add))
                    wait_past(dve, gathered[p], 256 * v)
                    ch.mark(dve.tensor_scalar(block_expert[0:1, p, :], bsum[:], float(NEXP - 1), None, ALU.min))
                    dve.tensor_copy(idx[:, p], pos[:]).then_inc(d_plan[p], 1)
                    yield

                if p == 0:
                    yield from places()
                    yield from other
                else:
                    yield from alternate(other, places())
                dve.wait_ge(d_exp[p], v + 1)
                yield from ch.link(dve.tensor_scalar(rs_t[:], ex[:], 2.0, 2.0, ALU.mult, ALU.add))
                yield from ch.link(dve.reciprocal(gate[:, p, 0, :], rs_t[:]))
                yield from ch.link(dve.tensor_tensor(gate[:, p, 1, :], gate[:, p, 0, :], ex[:], ALU.mult))
                assert ch.k == DISPATCH_STEPS, ch.k
                dve.wait_ge(d_plan[p], v + 1)
                step_past(dve, dve_past)

            def combine(v, p):
                w = served(v, p)
                ch = Chain(dve, c_chain[p], v * COMBINE_STEPS)
                dve.wait_ge(gathered[p], 256 * (v + 1))
                for i in range(TW):
                    ch.mark(dve.scalar_tensor_tensor(x_tile(w, i), yg[:, 0, i, :], gate[:, p, 0, i:i + 1],
                                                     x_tile(w, i), ALU.mult, ALU.add))
                    yield
                ch.settle()
                for i in range(TW):
                    dve.scalar_tensor_tensor(x_tile(w, i), yg[:, 1, i, :], gate[:, p, 1, i:i + 1],
                                             x_tile(w, i), ALU.mult, ALU.add).then_inc(c_x[p], 1)
                    yield
                dve.wait_ge(c_x[p], TW * (v + 1))
                step_past(dve, dve_past)
                assert ch.k == COMBINE_STEPS

            def prepare(v):
                ch = Chain(dve, m_chain, v * MIX0_STEPS)
                step_past(dve, dve_past)
                yield from moments(ch, v, mix_stats, mix_mv, mix_v)
                yield from rsqrt(ch, prep)
                y = mix_y[:].bitcast(F32)
                yield from ch.link(dve.tensor_copy(r1[:], y))
                yield from ch.link(dve.tensor_tensor(mix_t[:], r1[:], r1[:], ALU.mult))
                yield from ch.link(dve.tensor_tensor(mix_v[:], mix_t[:], mix_mv[:, :, 1], ALU.mult))
                yield from ch.link(dve.tensor_scalar(mix_v[:], mix_v[:], EPS, None, ALU.add))
                yield from rsqrt(ch, prep)
                yield from ch.link(dve.tensor_tensor(mix_h[:], r1[:], y, ALU.mult))
                for i in range(TW):
                    dve.tensor_scalar(un[:, i, :], x_tile(v, i), mix_mv[:, i, 0:1], mix_h[:, i:i + 1],
                                      ALU.subtract, ALU.mult).then_inc(m_u, 1)
                    yield
                yield from ch.link(dve.scalar_tensor_tensor(mix_t[:], mix_mv[:, :, 0], -1.0, r1[:], ALU.mult, ALU.mult))
                yield from ch.link(dve.tensor_scalar(mix_v[:], r1[:], 1.0, None, ALU.add))
                dve.wait_ge(m_u, TW * (v + 1))
                for i in range(TW):
                    ch.mark(dve.tensor_scalar(x_tile(v, i), x_tile(v, i), mix_v[:, i:i + 1], mix_t[:, i:i + 1],
                                              ALU.mult, ALU.add))
                    yield
                dve.wait_ge(m_dt, v + 1)
                raw = bank[7][:].rearrange("p (j c f) -> p c j f", j=BW, c=CH)[:, :, :, 64 - NHEADS:64]
                for c in range(CH):
                    ch.mark(dve.tensor_tensor(dtx[:, c], raw[:, c], dtb_sb[:].unsqueeze(1).broadcast_to([P, BW, NHEADS]),
                                              ALU.add))
                yield
                ch.settle()
                dve.scalar_tensor_tensor(dta[:], dtx[:], -1.0, dtx[:], ALU.mult, ALU.max).then_inc(m_abs, 1)
                yield
                dve.wait_ge(m_exp, v + 1)
                dve.tensor_scalar(dtu[:], dte[:], 1.0, None, ALU.add).then_inc(m_one, 1)
                yield
                dve.wait_ge(m_one, v + 1)
                ch.mark(dve.reciprocal(dtr[:], dtu[:]))
                yield from ch.link(dve.tensor_scalar(dta[:], dtu[:], -1.0, None, ALU.add))
                yield from ch.link(dve.scalar_tensor_tensor(dta[:], dta[:], -1.0, dte[:], ALU.mult, ALU.add))
                yield from ch.link(dve.tensor_tensor(dta[:], dta[:], dtr[:], ALU.mult))
                dve.wait_ge(m_log, v + 1)
                yield from ch.link(dve.tensor_tensor(dta[:], dta[:], dtl[:], ALU.add))
                yield from ch.link(dve.scalar_tensor_tensor(dt_t[:], dtx[:], 0.0, dta[:], ALU.max, ALU.add))
                dve.tensor_tensor(a_t[:].rearrange("p c j h -> p (c j) h"), dt_t[:].rearrange("p c j h -> p (c j) h"),
                                  aneg_sb[:].unsqueeze(1).broadcast_to([P, CH * BW, NHEADS]), ALU.mult).then_inc(m_a, 1)
                yield
                dve.wait_ge(m_cs, v + 1)
                wait_past(dve, b_decay, 8 * BW * v)
                sums = bank[6][:, 0:CH * BW * NHEADS]
                dve.tensor_copy(cs_t[:], sums).then_inc(m_cst, 1)
                yield from ch.link(dve.tensor_scalar(ncs_t[:].rearrange("p c j h -> p (c j h)"), sums, -1.0, None,
                                                     ALU.mult))
                step_past(dve, dve_past)
                assert ch.k == MIX0_STEPS, ch.k

            def prepare_weights():
                dve.wait_ge(weights_loaded, 16 * WEIGHT_DMAS)
                dve.wait_ge(fixed_act, 1)
                dve.tensor_scalar(aneg_sb[:], aneg_sb[:], -1.0, None, ALU.mult).then_inc(fixed_dve, 1)
                for m in range(2):
                    dve.tensor_scalar(w_out_sb[:, m, :], w_out_sb[:, m, :], normw_sb[:, m:m + 1], None,
                                      ALU.mult).then_inc(fixed_dve, 1)
                rest = b2_row
                for i in range(3):
                    if i:
                        dve.wait_ge(b2_split, 2 * i - 1)
                        dve.tensor_tensor(b2_rest, rest, b2_part[i - 1][:], ALU.subtract).then_inc(b2_split, 1)
                        dve.wait_ge(b2_split, 2 * i)
                        rest = b2_rest
                    dve.tensor_copy(b2_part[i][:], rest).then_inc(b2_split, 1)
                consts_ready(dve)

            def experts(v, p, done, sides):
                y_banks = Y_BANKS[p]

                def rows(b):
                    dve.wait_ge(e_Y[p], v * NB + b + 1)
                    s = b % RING
                    if b % GROUP == 0 and b >= RING:
                        dve.wait_ge(y_stored[p][s // GROUP], 16 * (ROUNDS * v + b // RING))
                    elif b % GROUP == 0:
                        for q in range(2):
                            wait_past(dve, y_stored[q][s // GROUP], 16 * ROUNDS * done[q])
                    dve.tensor_copy(yb[:, s, :], bank[y_banks[b % len(y_banks)]][:, 0:P]).then_inc(e_y[p], 1)

                for b in range(NB):
                    if b > 0:
                        rows(b)
                    for n in range(max(rate[b] for _, rate in sides)):
                        for side, rate in sides:
                            if n < rate[b]:
                                advance(side)
                    if b == 0:
                        rows(b)

            def convolve(w):
                for q in range(2):
                    for i in range(4):
                        k = 4 * q + i
                        dve.wait_ge(p_acc, 8 * w + k + 1)
                        a = acc[:, k % 3, :].rearrange("p (j t) -> p j t", j=2)
                        v = bank[PROJECT_BANKS[k % 3]][:].rearrange("p (j t) -> p j t", j=2)
                        for back in range(1, D_CONV):
                            if back > 1:
                                dve.wait_ge(p_older, 16 * w + 2 * k + back - 1)
                            ins = dve.scalar_tensor_tensor(
                                a[:, :, back:], v[:, :, :SEQ - back], conv_w_sb[:, i, D_CONV - 1 - back:D_CONV - back],
                                a[:, :, back:], ALU.mult, ALU.add)
                            ins.then_inc(p_older if back < D_CONV - 1 else p_tap, 1)
                            yield

            def mixer(w, side):
                def weights(j):
                    dve.wait_ge(b_T, BW * w + j + 1)
                    wait_past(dve, b_Y, BW * w + j - 1)
                    dve.tensor_tensor(xdt[:, j % 2], bank[0][:].rearrange("p (c h d) -> p c h d", c=CH, h=NHEADS),
                                      dt_t[:, :, j, :].unsqueeze(3).broadcast_to([P, CH, NHEADS, HEADDIM]),
                                      ALU.mult).then_inc(b_xdt, 1)
                    dve.wait_ge(b_G, BW * w + j + 1)
                    dve.tensor_tensor(gm[:, j % 2].rearrange("p a l -> p (a l)"), bank[1][:, 0:3 * P],
                                      causal[:].rearrange("p a l -> p (a l)"), ALU.mult).then_inc(b_gm, 1)
                    advance(side, WEIGHTS_SIDE[j][0])
                    dve.wait_ge(b_gm, BW * w + j + 1)
                    dve.wait_ge(b_decay, 8 * (BW * w + j + 1))
                    mixing = decay_view(decay[:, j % 2, :])
                    g = gm[:, j % 2].rearrange("p a l -> p (a l)")
                    for part, cols in ((0, slice(0, SEQ)), (1, slice(SEQ, 3 * P))):
                        n = cols.stop - cols.start
                        dve.scalar_tensor_tensor(mixing[part], mixing[part], 1.0,
                                                 g[:, cols].unsqueeze(1).broadcast_to([P, NHEADS, n]),
                                                 ALU.min, ALU.mult).then_inc(b_mix, 1)
                    advance(side, WEIGHTS_SIDE[j][1])

                def gated(j):
                    dve.wait_ge(b_Y, BW * w + j + 1)
                    wait_past(dve, b_O, BW * w + j - 1)
                    for m in range(2):
                        t = slice(SEQ * j, SEQ * j + SEQ)
                        ch.mark(dve.scalar_tensor_tensor(yz[:, j % 2, m, :], xbc[:, m, t], dskip_sb[:, m:m + 1],
                                                         bank[2 + j % 2][:, SEQ * m:SEQ * m + SEQ], ALU.mult, ALU.add))
                    advance(side, GATED_SIDE[j][0])
                    ch.settle()
                    dve.tensor_tensor(yz[:, j % 2], yz[:, j % 2], zs[:, :, SEQ * j:SEQ * j + SEQ],
                                      ALU.mult).then_inc(b_yz, 1)
                    advance(side, GATED_SIDE[j][1])

                ch = Chain(dve, b_chain, w * SCAN_STEPS)
                dve.wait_ge(p_zs, 4 * (w + 1))
                weights(0)
                for j in range(BW):
                    if j + 1 < BW:
                        weights(j + 1)
                    gated(j)
                assert ch.k == 2 * BW, ch.k

            def last_norm(w):
                ch = Chain(dve, b_chain, w * SCAN_STEPS + 2 * BW)
                dve.wait_ge(b_o, BW * (w + 1))
                sums = o_sb[:, :, 2 * D:].rearrange("p j (c e) -> p j c e", c=CH)[:, :, :, 0]
                yield from ch.link(dve.tensor_scalar(fin_v[:].rearrange("p (j c) -> p j c", j=BW), sums,
                                                     1.0 / D_INNER, EPS, ALU.mult, ALU.add))
                yield from rsqrt(ch, fin)
                y = fin_y[:].bitcast(F32)
                for i in range(TW):
                    dve.scalar_tensor_tensor(x_tile(w, i), o_sb[:, i // CH, D * (i % CH):D * (i % CH) + D],
                                             y[:, i:i + 1], x_tile(w, i), ALU.mult, ALU.add).then_inc(b_x, 1)
                    yield
                dve.wait_ge(b_x, TW * (w + 1))
                step_past(dve, dve_past)
                assert ch.k == SCAN_STEPS - 2 * BW, ch.k

            def step(k):
                late = route(k, 1, combine(k - 1, 1) if has(k - 2) else iter(range(2 * TW)))
                if has(k + 2):
                    early = route(k + 1, 0, combine(k, 0))
                else:
                    early = chain(iter(range(NORM + CHOICE + 1)), combine(k, 0), iter(range(3)))
                taps = convolve(k)
                experts(k, 0, (k, k), ((taps, TAP_RATE), (late, ROUTE_RATE), (early, NORM_RATE)))
                finish(taps)
                finish(late)
                mixer(k, early)
                norm = chain(iter(range(17)), last_norm(k))
                side = chain(early, alternate(prepare(k + 1), norm))
                experts(k, 1, (k + 1, k), ((side, PREPARE_RATE),))
                finish(side)

            def first_steps():
                first = route(0, 1, iter(()))
                advance(first, NORM)
                router_ready(dve)
                finish(first)
                prepare_weights()
                side = route(0, 0, iter(()))
                experts(0, 1, (0, 0), ((side, [20, 17, 0, 0, 7, 6, 17] + [0] * (NB - 7)),))
                finish(side)
                early = route(1, 0, combine(0, 0))
                side = chain(combine(0, 1), prepare(0))
                experts(0, 0, (0, 1), ((early, [20, 17, 0, 0, 7, 6, 5, 5, 4] + [0] * (NB - 9)),
                                       (side, [0] * 11 + [5] * 3 + [6, 7] + [6] * 2 + [8] * 5 + [0])))
                finish(side)
                finish(convolve(0))
                finish(early)
                side = prepare(1)
                mixer(0, side)
                advance(side, 37)
                finish(alternate(side, last_norm(0)))

            NORM, CHOICE = 2 * TW + 1 + RSQRT_STEPS + TW, 13 + 14
            WEIGHTS_SIDE = ((0, 0), (2, 4), (1, 2), (2, 2))
            GATED_SIDE = ((2, 2), (0, 0), (2, 2), (2, 4))
            assert sum(map(sum, WEIGHTS_SIDE + GATED_SIDE)) == CHOICE
            ROUTE_RATE = [6, 6, 4, 4, 3, 3, 3, 3, 3, 2, 0, 0, 0, 0, 3, 3, 4, 3, 0] + [6] * (NB - 19)
            TAP_RATE = [0, 0] + [2, 1] * 8 + [0] * (NB - 18)
            NORM_RATE = [0] * 10 + [4, 4, 4, 3, 3, 3, 3, 3, 3, 3, 2, 2] + [0] * (NB - 22)
            assert sum(NORM_RATE) == NORM
            PREPARE_RATE = [5] * 4 + [11, 11, 12, 8, 8, 8, 9, 9] + [4] * 6 + [5] * (NB - 18)

            def last_steps():
                k = NW - 1
                taps, late = convolve(k), route(k, 1, combine(k - 1, 1))
                for _ in range(8 * (D_CONV - 1)):
                    advance(taps)
                    advance(late)
                finish(taps)
                finish(late)
                mixer(k, iter(()))
                side = chain(last_norm(k), route(k, 0, iter(())))
                experts(k, 1, (k, k), ((side, [20, 20, 18, 0, 7, 6, 17] + [0] * (NB - 7)),))
                finish(side)
                side = combine(k, 1)
                experts(k, 0, (k, NW), ((side, [0] * 12 + [2] * TW + [0] * (NB - TW - 12)),))
                finish(side)
                finish(combine(k, 0))

            run_steps(dve, first_steps, step, last_steps)


def kernel(**inputs):
    import numpy as np
    import concourse.bacc as bacc
    from concourse.bass_utils import run_bass_kernel_spmd

    def col(v, m):
        v = np.asarray(v)
        return np.ascontiguousarray(np.moveaxis(v.reshape(m, P, *v.shape[1:]), 0, 1))

    a = {k.removeprefix("L0_"): np.asarray(v) for k, v in inputs.items()}
    arrays = {
        "x": a["attn_x"], "w_in_t": np.ascontiguousarray(a["attn_W_in"].T),
        "conv_w": col(a["attn_conv_w"], 4), "conv_b": col(a["attn_conv_b"], 4),
        "dt_bias": a["attn_dt_bias"], "a_log": a["attn_A_log"], "dskip": np.ascontiguousarray(a["attn_Dskip"].reshape(2, 2).T),
        "norm_w": col(a["attn_norm_w"], 2), "w_out_t": np.ascontiguousarray(a["attn_W_out"].T),
        "ln_g": a["attn_ln_g"].reshape(P, 1), "ln_b": a["attn_ln_b"].reshape(P, 1),
        "wr": a["ffn_Wr"], "br": a["ffn_br"], "w1": a["ffn_W1"],
        "b1": np.ascontiguousarray(a["ffn_b1"].reshape(NEXP, 2, P).transpose(2, 0, 1)),
        "w2": a["ffn_W2"], "b2": a["ffn_b2"],
    }
    nc = bacc.Bacc("TRN2", target_bir_lowering=False, num_devices=1)
    args = {n: nc.dram_tensor(f"in_{n}", v.shape, mybir.dt.from_np(v.dtype), kind="ExternalInput").ap()
            for n, v in arrays.items()}
    out = nc.dram_tensor("out", a["attn_x"].shape, F32, kind="ExternalOutput").ap()
    build_program(nc, out=out, **args)
    result = run_bass_kernel_spmd(nc, [{f"in_{n}": v for n, v in arrays.items()}], core_ids=[0])
    return result.results[0]["out"]
```
